# Optimizing a Trainium2 kernel written in Bass

```python
import numpy as np
import jax
import jax.numpy as jnp

def _softmax(x, axis=-1):
    return jax.nn.softmax(x, axis=axis)

def _gelu(x):
    return jax.nn.gelu(x, approximate=True)

def _silu(x):
    return jax.nn.silu(x)

def _sigmoid(x):
    return jax.nn.sigmoid(x)

def _layernorm(x, axis=-1, eps=1e-05):
    m = jnp.mean(x, axis=axis, keepdims=True)
    v = jnp.var(x, axis=axis, keepdims=True)
    return (x - m) / jnp.sqrt(v + eps)

def _scatter_add(tgt, idx, src, axis=0):
    return tgt.at[idx].add(src)

def _segment_sum(src, seg, n):
    return jax.ops.segment_sum(src, seg, n)
kernel_name = 'mk_gnn_preln_d2_gnn_r8_678772'

def setup_inputs(seed: int=0):
    np.random.seed(seed)
    _w = jnp.asarray

    def _rec_inputs():
        import jax
        import jax.numpy as jnp
        _gk = jax.random.key(seed)
        x = -0.0001006 + 1 * jax.random.normal(jax.random.fold_in(_gk, 1), (6250, 96), jnp.float32)
        src = jax.random.randint(jax.random.fold_in(_gk, 2), (200000,), 0, 6250, jnp.int32)
        dst = jnp.minimum((6250 * jax.random.uniform(jax.random.fold_in(_gk, 3), (200000,)) ** 2.0).astype(jnp.int32), 49999)
        _o = jnp.argsort(dst, stable=True)
        src = src[_o]
        dst = dst[_o]
        edge_attr_17 = jax.random.uniform(jax.random.fold_in(_gk, 11), (200000, 17), jnp.float32, 0.0, 1)
        return (x, src, dst, edge_attr_17)
    x, src, dst, edge_attr_17 = _rec_inputs()

    def _L0_gnn_setup():
        import jax, jax.numpy as jnp
        import numpy as np
        N = 6250
        E = 100000
        D = 96
        ED = 17
        key = jax.random.key(seed)
        ks = jax.random.split(key, 12)
        x = jax.random.normal(ks[0], (N, D), dtype=jnp.float32)
        edge_index = jax.random.randint(ks[1], (2, E), 0, N, dtype=jnp.int64)
        edge_attr = jax.random.uniform(ks[2], (E, ED), dtype=jnp.float32)
        s = 1.0 / np.sqrt(ED)
        W1 = jax.random.uniform(ks[3], (D, ED), jnp.float32, -s, s)
        b1 = jax.random.uniform(ks[4], (D,), jnp.float32, -s, s)
        s = 1.0 / np.sqrt(D)
        W2 = jax.random.uniform(ks[5], (D, D), jnp.float32, -s, s)
        b2 = jax.random.uniform(ks[6], (D,), jnp.float32, -s, s)
        Ws = jax.random.uniform(ks[7], (D, D), jnp.float32, -s, s)
        bs = jax.random.uniform(ks[8], (D,), jnp.float32, -s, s)
        Wn = jax.random.uniform(ks[9], (D, D), jnp.float32, -s, s)
        bn = jax.random.uniform(ks[10], (D,), jnp.float32, -s, s)
        return {'x': x, 'edge_index': edge_index, 'edge_attr': edge_attr, 'W1': W1, 'b1': b1, 'W2': W2, 'b2': b2, 'Ws': Ws, 'bs': bs, 'Wn': Wn, 'bn': bn}
    _L0_gnn_all = _L0_gnn_setup()
    _L0_gnn_in = {k: v for k, v in _L0_gnn_all.items() if k in ('W1', 'b1', 'W2', 'b2', 'Ws', 'bs', 'Wn', 'bn')}
    del _L0_gnn_all

    def _L1_gnn_setup():
        import jax, jax.numpy as jnp
        import numpy as np
        N_NODES = 6250
        N_EDGES = 100000
        D_IN = 96
        D_OUT = 96
        key = jax.random.key(seed)
        k1, k2, k3, k4 = jax.random.split(key, 4)
        x = jax.random.normal(k1, (N_NODES, D_IN), dtype=jnp.float32)
        edge_index = jax.random.randint(k2, (2, N_EDGES), 0, N_NODES, dtype=jnp.int64)
        W = jax.random.normal(k3, (D_IN, D_OUT), dtype=jnp.float32) * (1.0 / np.sqrt(D_IN))
        b = jax.random.normal(k4, (D_OUT,), dtype=jnp.float32) * 0.01
        return {'x': x, 'edge_index': edge_index, 'W': W, 'b': b}
    _L1_gnn_all = _L1_gnn_setup()
    _L1_gnn_in = {k: v for k, v in _L1_gnn_all.items() if k in ('W', 'b')}
    del _L1_gnn_all
    return {'x': x, 'src': src, 'dst': dst, 'edge_attr_17': edge_attr_17, 'L0_gnn_W1': _L0_gnn_in['W1'], 'L0_gnn_b1': _L0_gnn_in['b1'], 'L0_gnn_W2': _L0_gnn_in['W2'], 'L0_gnn_b2': _L0_gnn_in['b2'], 'L0_gnn_Ws': _L0_gnn_in['Ws'], 'L0_gnn_bs': _L0_gnn_in['bs'], 'L0_gnn_Wn': _L0_gnn_in['Wn'], 'L0_gnn_bn': _L0_gnn_in['bn'], 'L1_gnn_W': _L1_gnn_in['W'], 'L1_gnn_b': _L1_gnn_in['b']}

def reference(x, src, dst, edge_attr_17, L0_gnn_W1, L0_gnn_b1, L0_gnn_W2, L0_gnn_b2, L0_gnn_Ws, L0_gnn_bs, L0_gnn_Wn, L0_gnn_bn, L1_gnn_W, L1_gnn_b):
    import jax
    import jax.numpy as jnp

    def _L0_gnn_ref(x, edge_index, edge_attr, W1, b1, W2, b2, Ws, bs, Wn, bn):
        import jax, jax.numpy as jnp
        import numpy as np
        N = 6250
        E = 100000
        D = 96
        ED = 17
        src, dst = (edge_index[0], edge_index[1])
        h = jax.nn.relu(edge_attr @ W1.T + b1)
        w = h @ W2.T + b2
        msg = w * x[src]
        agg = jax.ops.segment_sum(msg, dst, num_segments=x.shape[0])
        return jax.nn.relu(x @ Ws.T + bs + agg @ Wn.T + bn)

    def _L1_gnn_ref(x, edge_index, W, b):
        import jax, jax.numpy as jnp
        import numpy as np
        N_NODES = 6250
        N_EDGES = 100000
        D_IN = 96
        D_OUT = 96
        num_nodes = x.shape[0]
        src, dst = (edge_index[0], edge_index[1])
        messages = x[src] @ W + b
        out = jax.ops.segment_sum(messages, dst, num_segments=num_nodes)
        deg = jax.ops.segment_sum(jnp.ones((dst.shape[0],), dtype=x.dtype), dst, num_segments=num_nodes)
        deg = jnp.clip(deg, 1.0, None)
        return out / deg[:, None]
    edge_index = jnp.stack([src, dst])
    h = jnp.maximum(_layernorm(x, axis=-1), 0.0)
    x = x + _L0_gnn_ref(h, edge_index, edge_attr_17, L0_gnn_W1, L0_gnn_b1, L0_gnn_W2, L0_gnn_b2, L0_gnn_Ws, L0_gnn_bs, L0_gnn_Wn, L0_gnn_bn)
    h = jnp.maximum(_layernorm(x, axis=-1), 0.0)
    x = x + _L1_gnn_ref(h, edge_index, L1_gnn_W, L1_gnn_b)
    return x

_drawn_inputs = setup_inputs


def setup_inputs(seed=0):
    import zlib

    import numpy as np

    out = dict(_drawn_inputs(seed))
    spreads = {}
    factors = {'L1_gnn_b': 8.0}
    for name, (base, spread) in spreads.items():
        noise = np.random.default_rng([zlib.crc32(name.encode()), seed]).standard_normal(out[name].shape)
        drawn = base * np.exp(spread * noise) if base else spread * noise
        out[name] = jnp.asarray(drawn.astype(out[name].dtype))
    for name, factor in factors.items():
        out[name] = (out[name] * factor).astype(out[name].dtype)
    return out
```

```python
from contextlib import ExitStack

import concourse.bass as bass
from concourse import mybir

F32 = mybir.dt.float32
I32 = mybir.dt.int32
ALU = mybir.AluOpType
ACT = mybir.ActivationFunctionType
AX = mybir.AxisListType

P = 128
N = 6250
E = 200000
D = 96
DE = 17
D1 = D + 1
TILES = -(-N // P)
LAST = N - (TILES - 1) * P
NPAD = TILES * P
J = 8
GE = J * P
GROUPS = -(-E // GE)
EPAD = GROUPS * GE
STEPS = GROUPS // 2
Q = 7
TURNS = TILES // Q
HALF = 512
BP = 98
EPS = 1e-5
assert GROUPS % 2 == 0 and TILES % Q == 0 and GROUPS % BP == 0


def gnn_program(nc, x, src_ids, dst_ids, dst_flat, edge_attr, w1t, b1, w2t, b2, wst, bs, wnt, bn, w, b, out):
    table = [nc.dram_tensor(f"node_table{n}", (NPAD, D1), F32, kind="Internal").ap() for n in range(2)]
    bounds_dram = nc.dram_tensor("bounds_dram", (GROUPS, 2), I32, kind="Internal").ap()

    with ExitStack() as ctx:
        def sb(name, shape, dt=F32):
            return ctx.enter_context(nc.sbuf_tensor(name, shape, dt))

        def sem(name):
            return ctx.enter_context(nc.semaphore(name))

        x_sb = sb("x_sb", [P, TILES, D])
        xc = sb("xc", [P, TILES, D])
        h_sb = sb("h_sb", [P, TILES, D1])
        acc = sb("acc", [P, TILES, D1])
        stat = sb("stat", [P, 4, TILES])
        dst_i = sb("dst_i", [P, GROUPS * J], I32)
        dst_f = sb("dst_f", [P, GROUPS * J])
        dst_b = sb("dst_b", [BP, GROUPS // BP, GE], I32)
        bnd = sb("bnd", [BP, GROUPS // BP, 2], I32)
        bounds = sb("bounds", [1, GROUPS * 2], I32)
        node_no = sb("node_no", [P, NPAD])
        ident = sb("ident", [P, P])
        idx = [sb(f"idx{s}", [P, J], I32) for s in range(2)]
        gat = [sb(f"gat{s}", [P, J, D1]) for s in range(2)]
        ea = [sb(f"ea{s}", [DE, GE]) for s in range(2)]
        hid = sb("hid", [D1, GE])
        msg = sb("msg", [P, J, D])
        onehot = sb("onehot", [P, J, P])
        stage_h = sb("stage_h", [P, Q, D1])
        stage_a = sb("stage_a", [P, Q, D1])
        ht = sb("ht", [D1, Q, P])
        at = sb("at", [D1, Q, P])
        w1t_sb = sb("w1t_sb", [DE, D])
        b1_sb = sb("b1_sb", [D, 1])
        w2t_sb = sb("w2t_sb", [D1, D])
        wst_sb = sb("wst_sb", [D1, D])
        wnt_sb = sb("wnt_sb", [D1, D])
        w_sb = sb("w_sb", [D1, D])

        hid_ps = ctx.enter_context(nc.psum_tensor("hid_ps", [P, 2 * HALF], F32))
        w_ps = ctx.enter_context(nc.psum_tensor("w_ps", [P, J, P], F32))
        agg_ps = ctx.enter_context(nc.psum_tensor("agg_ps", [P, HALF], F32))
        node_ps = ctx.enter_context(nc.psum_tensor("node_ps", [P, J, P], F32))
        ht_ps = hid_ps[:, :].rearrange("p (q n) -> p q n", n=P)
        at_ps = w_ps

        x_zeroed = sem("x_zeroed")
        x_in = sem("x_in")
        dst_in = sem("dst_in")
        dstb_in = sem("dstb_in")
        weights_in = sem("weights_in")
        bounds_out = sem("bounds_out")
        bounds_in = sem("bounds_in")
        pool_consts = sem("pool_consts")
        bounds_ready = sem("bounds_ready")
        ones_ready = sem("ones_ready")
        dve_done = sem("dve_done")
        var_ready = sem("var_ready")
        std_ready = sem("std_ready")
        h_ready = sem("h_ready")
        table_out = sem("table_out")
        idx_in = [sem(f"idx_in{s}") for s in range(2)]
        ea_in = [sem(f"ea_in{s}") for s in range(2)]
        gat_in = [sem(f"gat_in{s}") for s in range(2)]
        gat_free = [sem(f"gat_free{s}") for s in range(2)]
        hid_done = sem("hid_done")
        relu_done = sem("relu_done")
        w_done = sem("w_done")
        msg_done = sem("msg_done")
        onehot_done = sem("onehot_done")
        agg_done = sem("agg_done")
        acc_added = sem("acc_added")
        layer_done = sem("layer_done")
        stage_done = sem("stage_done")
        trans_done = sem("trans_done")
        copied = sem("copied")
        node_done = sem("node_done")
        node_used = sem("node_used")
        out_ready = sem("out_ready")
        out_written = sem("out_written")

        block = ctx.enter_context(nc.Block())

        def nodes(t):
            return t.rearrange("(t p) d -> p t d", p=P)

        @block.sync
        def _(sp):
            sp.wait_ge(x_zeroed, 1)
            sp.dma_start(x_sb[:, 0:TILES - 1, :], nodes(x[0:(TILES - 1) * P, :])).then_inc(x_in, 16)
            sp.dma_start(x_sb[0:LAST, TILES - 1, :], x[(TILES - 1) * P:N, :]).then_inc(x_in, 16)
            sp.dma_start(dst_b[:, :, :], dst_flat.rearrange("(p q e) -> p q e", p=BP, e=GE)).then_inc(dstb_in, 16)
            sp.dma_start(dst_i[:, :], dst_ids).then_inc(dst_in, 16)
            for tile, array in ((w1t_sb[:, :], w1t), (b1_sb[:, :], b1), (w2t_sb[0:D, :], w2t), (w2t_sb[D:D1, :], b2),
                                (wst_sb[0:D, :], wst), (wst_sb[D:D1, :], bs), (wnt_sb[0:D, :], wnt),
                                (wnt_sb[D:D1, :], bn), (w_sb[0:D, :], w), (w_sb[D:D1, :], b)):
                sp.dma_start(tile, array).then_inc(weights_in, 16)
            sp.wait_ge(bounds_ready, 1)
            sp.dma_start(bounds_dram.rearrange("(p q) c -> p q c", p=BP), bnd[:, :, :]).then_inc(bounds_out, 16)
            sp.wait_ge(bounds_out, 16)
            sp.dma_start(bounds[:, :], bounds_dram.rearrange("g c -> (g c)").rearrange("(a n) -> a n", a=1)).then_inc(bounds_in, 16)
            for layer in range(2):
                sp.wait_ge(h_ready, layer + 1)
                sp.dma_start(nodes(table[layer]), h_sb[:, :, :]).then_inc(table_out, 16)
                with sp.Fori(0, STEPS) as it:
                    for s in range(2):
                        g = it * 2 + s
                        if layer == 0:
                            sp.wait_ge(hid_done, g * 2 + 2)
                            sp.dma_start(ea[s][:, :], edge_attr[bass.ds(g, 1), :, :].rearrange("g c e -> (g c) e")).then_inc(ea_in[s], 16)
                        sp.wait_ge(gat_free[s], it + (layer * STEPS + 1))
                        sp.dma_start(idx[s][:, :], src_ids[bass.ds(g, 1), :, :].rearrange("g p j -> (g p) j")).then_inc(idx_in[s], 16)
            sp.wait_ge(out_ready, 1)
            sp.dma_start(nodes(out[0:(TILES - 1) * P, :]), xc[:, 0:TILES - 1, :]).then_inc(out_written, 16)
            sp.dma_start(out[(TILES - 1) * P:N, :], xc[0:LAST, TILES - 1, :]).then_inc(out_written, 16)
            sp.wait_ge(out_written, 32)

        @block.gpsimd
        def _(pool):
            pool.iota(node_no[:, :], [[1, NPAD]], base=0, channel_multiplier=0,
                      allow_small_or_imprecise_dtypes=True).then_inc(pool_consts, 1)
            pool.memset(ident[:, :], 0.0).then_inc(pool_consts, 1)
            pool.wait_ge(pool_consts, 2)
            pool.affine_select(out=ident[:, :], in_=ident[:, :], compare_op=ALU.not_equal, fill=1.0, base=0,
                               pattern=[[-1, P]], channel_multiplier=1).then_inc(pool_consts, 1)
            for s in range(2):
                pool.sem_inc(gat_free[s], 1)
            for layer in range(2):
                pool.wait_ge(table_out, 16 * (layer + 1))
                with pool.Fori(0, STEPS) as it:
                    for s in range(2):
                        pool.wait_ge(gat_free[s], it + (layer * STEPS + 1))
                        pool.nop(nofuse=True)
                        pool.wait_ge(idx_in[s], it * 16 + (16 * layer * STEPS + 16))
                        pool.nop(nofuse=True)
                        for j in range(J):
                            pool.indirect_dma_start(gat[s][:, j, :], None, table[layer],
                                                    bass.IndirectOffsetOnAxis(ap=idx[s][:, j:j + 1], axis=0)).then_inc(gat_in[s], 16)

        @block.scalar
        def _(act):
            act.sem_inc(relu_done, 2)

            def root(n):
                act.wait_ge(var_ready, n + 1)
                nc.scalar.activation(stat[:, 2, :], stat[:, 1, :], ACT.Sqrt).then_inc(std_ready, 1)

            def to_sbuf(turns_before, both):
                with act.Fori(0, TURNS) as it:
                    act.wait_ge(trans_done, it + (turns_before + 1))
                    act.wait_ge(node_done, it + (turns_before + 1))
                    if both:
                        nc.scalar.activation(ht[:, :, :], ht_ps[0:D1, 0:Q, :], ACT.Copy)
                    nc.scalar.activation(at[:, :, :], at_ps[0:D1, 0:Q, :], ACT.Copy).then_inc(copied, 1)

            root(0)
            act.wait_ge(weights_in, 160)
            act.wait_ge(ones_ready, 1)
            with act.Fori(0, GROUPS) as g:
                for half in range(2):
                    act.wait_ge(hid_done, g * 2 + (half + 5))
                    if half == 0:
                        act.wait_ge(w_done, g + 1)
                    cols = slice(half * HALF, (half + 1) * HALF)
                    nc.scalar.activation(hid[0:D, cols], hid_ps[0:D, cols], ACT.Relu, bias=b1_sb[:, :]).then_inc(relu_done, 1)
            to_sbuf(0, True)
            root(1)
            to_sbuf(TURNS, False)

        @block.tensor
        def _(pe):
            pe.sem_inc(hid_done, 4)
            pe.sem_inc(w_done, 1)
            pe.sem_inc(node_done, 1)
            pe.wait_ge(weights_in, 160)
            pe.wait_ge(pool_consts, 3)
            pe.wait_ge(bounds_in, 16)
            pairs = pe.alloc_register("pe_pairs")
            pe.reg_mov(pairs, 0)

            def aggregate(layer, g, rhs, width):
                first = pe.value_load(bounds[0:1, bass.ds(g * 2, 1)], min_val=0, max_val=TILES - 1)
                end = pe.value_load(bounds[0:1, bass.ds(g * 2 + 1, 1)], min_val=1, max_val=TILES)
                with pe.Fori(first, end) as blk:
                    n = pe.snap(pairs)
                    pe.wait_ge(onehot_done, n + 1)
                    pe.wait_ge(acc_added, n + 1)
                    for j in range(J):
                        last = nc.tensor.matmul(agg_ps[:, 0:width], onehot[:, j, :], rhs[:, j, :], start=(j == 0), stop=(j == J - 1))
                    last.then_inc(agg_done, 1)
                    pe.reg_add(pairs, pairs, 1)

            with pe.Fori(0, STEPS) as it:
                for s in range(2):
                    g = it * 2 + s
                    pe.wait_ge(ea_in[s], it * 16 + 16)
                    for half in range(2):
                        pe.wait_ge(relu_done, g * 2 + (half + 1))
                        cols = slice(half * HALF, (half + 1) * HALF)
                        last = nc.tensor.matmul(hid_ps[0:D, cols], w1t_sb[:, :], ea[s][:, cols], start=True, stop=True)
                        last.then_inc(hid_done, 1)
                    pe.wait_ge(msg_done, g + 1)
                    for half in range(2):
                        pe.wait_ge(relu_done, g * 2 + (half + 3))
                        for j in range(half * J // 2, (half + 1) * J // 2):
                            last = nc.tensor.matmul(w_ps[:, j, 0:D], hid[:, j * P:(j + 1) * P], w2t_sb[:, :], start=True, stop=True)
                    last.then_inc(w_done, 1)
                    pe.wait_ge(msg_done, g + 2)
                    aggregate(0, g, msg, D)

            with pe.Fori(0, TURNS) as it:
                pe.wait_ge(stage_done, it + 1)
                for q in range(Q):
                    nc.tensor.transpose(ht_ps[0:D1, q, :], stage_h[:, q, :], ident[:, :])
                    last = nc.tensor.transpose(at_ps[0:D1, q, :], stage_a[:, q, :], ident[:, :])
                last.then_inc(trans_done, 1)
                pe.wait_ge(copied, it + 1)
                pe.wait_ge(node_used, it + 1)
                for q in range(Q):
                    nc.tensor.matmul(node_ps[:, q, 0:D], ht[:, q, :], wst_sb[:, :], start=True, stop=False)
                    last = nc.tensor.matmul(node_ps[:, q, 0:D], at[0:D, q, :], wnt_sb[0:D, :], start=False, stop=True)
                last.then_inc(node_done, 1)

            with pe.Fori(0, STEPS) as it:
                for s in range(2):
                    g = it * 2 + s
                    pe.wait_ge(gat_in[s], it * (16 * J) + (16 * J * (STEPS + 1)))
                    aggregate(1, g, gat[s], D1)

            with pe.Fori(0, TURNS) as it:
                pe.wait_ge(stage_done, it + (TURNS + 1))
                for q in range(Q):
                    last = nc.tensor.transpose(at_ps[0:D1, q, :], stage_a[:, q, :], ident[:, :])
                last.then_inc(trans_done, 1)
                pe.wait_ge(copied, it + (TURNS + 1))
                pe.wait_ge(node_used, it + (TURNS + 1))
                for q in range(Q):
                    last = nc.tensor.matmul(node_ps[:, q, 0:D], at[:, q, :], w_sb[:, :], start=True, stop=True)
                last.then_inc(node_done, 1)

        @block.vector
        def _(dve):
            steps = [0]

            def step(ins):
                steps[0] += 1
                ins.then_inc(dve_done, 1)
                dve.wait_ge(dve_done, steps[0])

            def bcast(a):
                return a.unsqueeze(2).to_broadcast([P, TILES, D])

            def layernorm(n):
                step(nc.vector.reduce_sum(stat[:, 0, :], x_sb[:, :, :], axis=AX.X))
                step(nc.vector.tensor_single_scalar(stat[:, 0, :], stat[:, 0, :], 1.0 / D, ALU.mult))
                step(nc.vector.tensor_tensor(xc[:, :, :], x_sb[:, :, :], bcast(stat[:, 0, :]), ALU.subtract))
                step(nc.vector.tensor_tensor(h_sb[:, :, 0:D], xc[:, :, :], xc[:, :, :], ALU.mult))
                step(nc.vector.reduce_sum(stat[:, 1, :], h_sb[:, :, 0:D], axis=AX.X))
                nc.vector.tensor_scalar(stat[:, 1, :], stat[:, 1, :], 1.0 / D, EPS, ALU.mult, ALU.add).then_inc(var_ready, 1)
                dve.wait_ge(std_ready, n + 1)
                step(nc.vector.reciprocal(stat[:, 3, :], stat[:, 2, :]))
                nc.vector.scalar_tensor_tensor(h_sb[:, :, 0:D], xc[:, :, :], 0.0, bcast(stat[:, 3, :]), ALU.max, ALU.mult).then_inc(h_ready, 1)

            def aggregate(g, pairs, width):
                first = dve.value_load(bounds[0:1, bass.ds(g * 2, 1)], min_val=0, max_val=TILES - 1)
                end = dve.value_load(bounds[0:1, bass.ds(g * 2 + 1, 1)], min_val=1, max_val=TILES)
                ids = dst_f[:, bass.ds(g * J, J)].unsqueeze(2).to_broadcast([P, J, P])
                with dve.Fori(first, end) as blk:
                    n = dve.snap(pairs)
                    nos = node_no[:, bass.ds(blk * P, P)].unsqueeze(1).to_broadcast([P, J, P])
                    nc.vector.tensor_tensor(onehot[:, :, :], nos, ids, ALU.is_equal).then_inc(onehot_done, 1)
                    dve.wait_ge(acc_added, n + 1)
                    dve.wait_ge(agg_done, n + 1)
                    acc_blk = acc[:, bass.ds(blk, 1), 0:width].rearrange("p a d -> p (a d)")
                    nc.vector.tensor_tensor(acc_blk, acc_blk, agg_ps[:, 0:width], ALU.add).then_inc(acc_added, 1)
                    dve.reg_add(pairs, pairs, 1)

            nc.vector.memset(x_sb[:, TILES - 1, :], 0.0).then_inc(x_zeroed, 1)
            nc.vector.memset(hid[D:D1, :], 1.0).then_inc(ones_ready, 1)
            step(nc.vector.memset(h_sb[:, :, D:D1], 1.0))
            nc.vector.memset(acc[:, :, :], 0.0).then_inc(acc_added, 1)
            dve.wait_ge(dstb_in, 16)
            step(nc.vector.tensor_reduce(bnd[:, :, 0], dst_b[:, :, :], axis=AX.X, op=ALU.min))
            step(nc.vector.tensor_reduce(bnd[:, :, 1], dst_b[:, :, :], axis=AX.X, op=ALU.max))
            step(nc.vector.tensor_single_scalar(bnd[:, :, :], bnd[:, :, :], 7, ALU.logical_shift_right))
            nc.vector.tensor_single_scalar(bnd[:, :, 1], bnd[:, :, 1], 1, ALU.add).then_inc(bounds_ready, 1)
            dve.wait_ge(dst_in, 16)
            step(nc.vector.tensor_copy(dst_f[:, :], dst_i[:, :]))
            dve.wait_ge(x_in, 32)
            layernorm(0)

            dve.wait_ge(weights_in, 160)
            step(nc.vector.tensor_tensor(wst_sb[D:D1, :], wst_sb[D:D1, :], wnt_sb[D:D1, :], ALU.add))
            dve.wait_ge(bounds_in, 16)
            dve.wait_ge(pool_consts, 1)
            pairs = dve.alloc_register("dve_pairs")
            dve.reg_mov(pairs, 0)
            dve.sem_inc(msg_done, 1)
            with dve.Fori(0, STEPS) as it:
                for s in range(2):
                    g = it * 2 + s
                    dve.wait_ge(gat_in[s], it * (16 * J) + 16 * J)
                    dve.wait_ge(w_done, g + 2)
                    nc.vector.tensor_tensor(msg[:, :, :], w_ps[:, :, 0:D], gat[s][:, :, 0:D], ALU.mult).then_inc(msg_done, 1)
                    dve.wait_ge(msg_done, g + 2)
                    dve.sem_inc(gat_free[s], 1)
                    aggregate(g, pairs, D)
            n = dve.snap(pairs)
            dve.wait_ge(acc_added, n + 1)

            dve.sem_inc(node_used, 1)
            with dve.Fori(0, TURNS) as it:
                dve.wait_ge(node_done, it + 1)
                nc.vector.tensor_copy(stage_h[:, :, :], h_sb[:, bass.ds(it * Q, Q), :])
                nc.vector.tensor_copy(stage_a[:, :, :], acc[:, bass.ds(it * Q, Q), :]).then_inc(stage_done, 1)
                dve.wait_ge(node_done, it + 2)
                tiles = x_sb[:, bass.ds(it * Q, Q), :]
                nc.vector.scalar_tensor_tensor(tiles, node_ps[:, 0:Q, 0:D], 0.0, tiles, ALU.max, ALU.add).then_inc(node_used, 1)
            dve.wait_ge(node_used, TURNS + 1)
            step(nc.vector.memset(acc[:, :, :], 0.0))
            layernorm(1)

            with dve.Fori(0, STEPS) as it:
                for s in range(2):
                    g = it * 2 + s
                    aggregate(g, pairs, D1)
                    n = dve.snap(pairs)
                    dve.wait_ge(agg_done, n)
                    dve.sem_inc(gat_free[s], 1)
            n = dve.snap(pairs)
            dve.wait_ge(acc_added, n + 1)

            step(nc.vector.tensor_single_scalar(stat[:, 0, :], acc[:, :, D], 1.0, ALU.max))
            step(nc.vector.reciprocal(stat[:, 1, :], stat[:, 0, :]))
            with dve.Fori(0, TURNS) as it:
                dve.wait_ge(node_done, it + (TURNS + 1))
                nc.vector.tensor_copy(stage_a[:, :, :], acc[:, bass.ds(it * Q, Q), :]).then_inc(stage_done, 1)
                dve.wait_ge(node_done, it + (TURNS + 2))
                o = xc[:, bass.ds(it * Q, Q), :]
                r = stat[:, 1, bass.ds(it * Q, Q)].unsqueeze(2).to_broadcast([P, Q, D])
                nc.vector.tensor_tensor(o, node_ps[:, 0:Q, 0:D], r, ALU.mult).then_inc(node_used, 1)
            dve.wait_ge(node_used, 2 * TURNS + 1)
            nc.vector.tensor_tensor(xc[:, :, :], xc[:, :, :], x_sb[:, :, :], ALU.add).then_inc(out_ready, 1)


def kernel(x, src, dst, edge_attr_17, L0_gnn_W1, L0_gnn_b1, L0_gnn_W2, L0_gnn_b2, L0_gnn_Ws, L0_gnn_bs,
           L0_gnn_Wn, L0_gnn_bn, L1_gnn_W, L1_gnn_b):
    import numpy as np
    import concourse.bacc as bacc
    from concourse.bass_utils import run_bass_kernel_spmd

    def padded(a, fill):
        return np.concatenate([np.asarray(a), np.full((EPAD - E, *a.shape[1:]), fill, np.asarray(a).dtype)])

    src_p = padded(src, 0).reshape(GROUPS, J, P)
    dst_p = padded(dst, NPAD - 1)
    ea_p = padded(edge_attr_17, 0).reshape(GROUPS, GE, DE)
    arrays = {
        "x": x,
        "src_ids": src_p.transpose(0, 2, 1),
        "dst_ids": dst_p.reshape(GROUPS * J, P).T,
        "dst_flat": dst_p,
        "edge_attr": ea_p.transpose(0, 2, 1),
        "w1t": np.asarray(L0_gnn_W1).T, "b1": np.asarray(L0_gnn_b1).reshape(D, 1),
        "w2t": np.asarray(L0_gnn_W2).T, "b2": np.asarray(L0_gnn_b2).reshape(1, D),
        "wst": np.asarray(L0_gnn_Ws).T, "bs": np.asarray(L0_gnn_bs).reshape(1, D),
        "wnt": np.asarray(L0_gnn_Wn).T, "bn": np.asarray(L0_gnn_bn).reshape(1, D),
        "w": L1_gnn_W, "b": np.asarray(L1_gnn_b).reshape(1, D),
    }
    nc = bacc.Bacc("TRN2", target_bir_lowering=False, num_devices=1)
    arrays = {k: np.ascontiguousarray(v) for k, v in arrays.items()}
    aps = [nc.dram_tensor(k, v.shape, mybir.dt.from_np(v.dtype), kind="ExternalInput").ap() for k, v in arrays.items()]
    out = nc.dram_tensor("out", (N, D), F32, kind="ExternalOutput").ap()
    gnn_program(nc, *aps, out)
    return run_bass_kernel_spmd(nc, [arrays], core_ids=[0]).results[0]["out"]
```

```python
from contextlib import ExitStack

import concourse.bass as bass
from concourse import mybir

F32 = mybir.dt.float32
BF16 = mybir.dt.bfloat16
I32 = mybir.dt.int32
ALU = mybir.AluOpType
ACT = mybir.ActivationFunctionType
AX = mybir.AxisListType

P = 128
N = 6250
E = 200000
D = 96
DE = 17
D1 = D + 1
R = 3
PW = R * D1 + 1
TILES = -(-N // P)
LAST = N - (TILES - 1) * P
NPAD = TILES * P
Q = 7
TURNS = TILES // Q
J = 8
GE = J * P
GROUPS = -(-E // GE)
EPAD = GROUPS * GE
S = 4
STEPS = GROUPS // S
W = 96
WMAX = -(-NPAD // W)
HALF = 512
BP = 98
BQ = GROUPS // BP
EPS = 1e-5
assert GROUPS % S == 0 and TILES % Q == 0 and GROUPS % BP == 0


def after(it, wraps=0):
    return it + (2 + wraps)


def gnn_program(nc, x, src_ids, dst_ids, dst_flat, edge_attr, w1t, b1, w2t, b2, wst, bs, wnt, bn, w, b, out):
    table = [nc.dram_tensor("node_table0", (NPAD, D), F32, kind="Internal").ap(),
             nc.dram_tensor("node_table1", (NPAD, PW), BF16, kind="Internal").ap()]
    bounds_dram = nc.dram_tensor("bounds_dram", (3, GROUPS), I32, kind="Internal").ap()

    with ExitStack() as ctx:
        def sb(name, shape, dt=F32):
            return ctx.enter_context(nc.sbuf_tensor(name, shape, dt))

        def sem(name):
            return ctx.enter_context(nc.semaphore(name))

        def slots(name):
            return [sem(f"{name}{s}") for s in range(S)]

        x_sb = sb("x_sb", [P, TILES, D])
        xc = sb("xc", [P, TILES, D])
        h_sb = sb("h_sb", [P, TILES, D1])
        parts1_rows = sb("parts1_rows", [P, TILES, PW], BF16)
        parts1 = parts1_rows[:, :, 0:R * D1].rearrange("p t (r d) -> p t r d", r=R)
        root = xc
        stat = sb("stat", [P, 4, TILES])
        acc = [sb(f"acc{n}", [D1, NPAD + W]) for n in range(2)]
        rel = sb("rel", [P, GROUPS, J])
        base_i = sb("base_i", [P, GROUPS], I32)
        base_f = sb("base_f", [P, GROUPS])
        bnd = sb("bnd", [BP, 3, BQ], I32)
        bounds = sb("bounds", [1, 3 * GROUPS], I32)
        dst_i = xc[:, :, :].rearrange("p t d -> p (t d)")[:, 0:GROUPS * J].bitcast(I32)
        dst_b = parts1_rows[0:BP, :, :].rearrange("p t d -> p (t d)")[:, 0:2 * BQ * GE].bitcast(I32)\
            .rearrange("p (q e) -> p q e", e=GE)
        iota = sb("iota", [P, W])
        ident = sb("ident", [P, P])
        idx = [sb(f"idx{s}", [P, J], I32) for s in range(S)]
        gat1 = [sb(f"gat{s}", [P, J, PW], BF16) for s in range(S)]
        gat0 = [t[:, :, :].rearrange("p j d -> p (j d)")[:, 0:2 * J * D].bitcast(F32).rearrange("p (j d) -> p j d", d=D)
                for t in gat1]
        ea = [sb(f"ea{s}", [DE, GE]) for s in range(S)]
        hid = sb("hid", [D1, GE])
        msg = sb("msg", [P, J, D])
        rest = sb("rest", [P, J, D])
        parts0 = [sb(f"parts0_{u}", [P, J, R, D], BF16) for u in range(2)]
        onehot = [sb(f"onehot{u}", [P, J, W], BF16) for u in range(2)]
        x_rel = sb("x_rel", [P, J])
        x_onehot = sb("x_onehot", [P, J, W], BF16)
        stage = parts0[0][:, :, :, :].rearrange("p j r d -> p (j r d)")[:, 0:2 * Q * D1].bitcast(F32)\
            .rearrange("p (q d) -> p q d", d=D1)
        shifts = sb("shifts", [P, WMAX])
        at = parts0[1][0:D1, :, :, :].rearrange("p j r d -> p (j r d)")[:, 0:2 * Q * P].bitcast(F32)\
            .rearrange("p (q n) -> p q n", n=P)
        w1t_sb = sb("w1t_sb", [DE, D])
        b1_sb = sb("b1_sb", [D, 1])
        w2t_sb = sb("w2t_sb", [D1, D])
        wst_sb = sb("wst_sb", [D1, D])
        wnt_sb = sb("wnt_sb", [D1, D])
        w_sb = sb("w_sb", [D1, D1])

        hid_ps = ctx.enter_context(nc.psum_tensor("hid_ps", [P, 2 * HALF], F32))
        w_ps = ctx.enter_context(nc.psum_tensor("w_ps", [P, J, P], F32))
        agg_ps = [ctx.enter_context(nc.psum_tensor(f"agg_ps{u}", [P, HALF], F32)) for u in range(2)]
        node_ps = ctx.enter_context(nc.psum_tensor("node_ps", [P, J, P], F32))
        at_ps = w_ps

        x_zeroed = sem("x_zeroed")
        x_in = sem("x_in")
        dst_in = sem("dst_in")
        dstb_in = sem("dstb_in")
        weights_in = sem("weights_in")
        bounds_ready = sem("bounds_ready")
        bounds_out = sem("bounds_out")
        bounds_in = sem("bounds_in")
        base_in = sem("base_in")
        pool_consts = sem("pool_consts")
        dve_consts = sem("dve_consts")
        dve_step = sem("dve_step")
        var_ready = sem("var_ready")
        std_ready = sem("std_ready")
        h_ready = sem("h_ready")
        table_parts = sem("table_parts")
        table_ready = sem("table_ready")
        table_out = sem("table_out")
        acc_ready = sem("acc_ready")
        idx_in = slots("idx_in")
        ea_in = slots("ea_in")
        gat_in = slots("gat_in")
        hid_done = [slots("hid_done_a"), slots("hid_done_b")]
        relu_done = [slots("relu_done_a"), slots("relu_done_b")]
        w_done = slots("w_done")
        msg_done = slots("msg_done")
        part1_done = slots("part1_done")
        rest_done = slots("rest_done")
        part2_done = slots("part2_done")
        part3_done = slots("part3_done")
        onehot_done = slots("onehot_done")
        agg_done = slots("agg_done")
        added = slots("added")
        x_rel_done = sem("x_rel_done")
        x_onehot_done = sem("x_onehot_done")
        x_agg_done = sem("x_agg_done")
        x_added = sem("x_added")
        stage_done = sem("stage_done")
        trans_done = sem("trans_done")
        copied = sem("copied")
        node_done = sem("node_done")
        node_used = sem("node_used")
        x_updated = sem("x_updated")
        scaled = sem("scaled")
        out_ready = sem("out_ready")
        out_written = sem("out_written")

        block = ctx.enter_context(nc.Block())

        def nodes(t):
            return t.rearrange("(t p) d -> p t d", p=P)

        @block.sync
        def _(sp):
            sp.dma_start(dst_b, dst_flat.rearrange("(p q e) -> p q e", p=BP, e=GE)).then_inc(dstb_in, 16)
            sp.wait_ge(x_zeroed, 1)
            sp.dma_start(x_sb[:, 0:TILES - 1, :], nodes(x[0:(TILES - 1) * P, :])).then_inc(x_in, 16)
            sp.dma_start(x_sb[0:LAST, TILES - 1, :], x[(TILES - 1) * P:N, :]).then_inc(x_in, 16)
            sp.dma_start(dst_i, dst_ids).then_inc(dst_in, 16)
            for tile, array in ((w1t_sb[:, :], w1t), (b1_sb[:, :], b1), (w2t_sb[0:D, :], w2t), (w2t_sb[D:D1, :], b2),
                                (wst_sb[0:D, :], wst), (wst_sb[D:D1, :], bs), (wnt_sb[0:D, :], wnt),
                                (wnt_sb[D:D1, :], bn), (w_sb[0:D, 0:D], w), (w_sb[D:D1, 0:D], b)):
                sp.dma_start(tile, array).then_inc(weights_in, 16)
            for group in (*hid_done, *relu_done, w_done, msg_done, part1_done, rest_done, part2_done, part3_done,
                          onehot_done, agg_done, added):
                for slot in group:
                    sp.sem_inc(slot, 1)
            sp.wait_ge(bounds_ready, 1)
            sp.dma_start(bounds_dram.rearrange("c (p q) -> p c q", p=BP), bnd[:, :, :]).then_inc(bounds_out, 16)
            sp.wait_ge(bounds_out, 16)
            sp.dma_start(bounds[:, :], bounds_dram.rearrange("c g -> (c g)").rearrange("(a n) -> a n", a=1)).then_inc(bounds_in, 16)
            sp.dma_start(base_i[:, :], bounds_dram[0:1, :].to_broadcast([P, GROUPS])).then_inc(base_in, 16)

            sp.wait_ge(h_ready, 1)
            sp.dma_start(nodes(table[0]), h_sb[:, :, 0:D]).then_inc(table_out, 16)
            with sp.Fori(0, STEPS) as it:
                for s in range(S):
                    g = it * S + s
                    sp.wait_ge(hid_done[1][s], after(it, -1))
                    sp.dma_start(ea[s][:, :], edge_attr[bass.ds(g, 1), :, :].rearrange("g c e -> (g c) e")).then_inc(ea_in[s], 16)
                    sp.wait_ge(msg_done[s], after(it, -1))
                    sp.dma_start(idx[s][:, :], src_ids[bass.ds(g, 1), :, :].rearrange("g p j -> (g p) j")).then_inc(idx_in[s], 16)
            sp.wait_ge(table_ready, 1)
            sp.dma_start(nodes(table[1]), parts1_rows[:, :, :]).then_inc(table_out, 16)
            with sp.Fori(0, STEPS) as it:
                for s in range(S):
                    g = it * S + s
                    sp.wait_ge(agg_done[s], after(it, STEPS - 1))
                    sp.dma_start(idx[s][:, :], src_ids[bass.ds(g, 1), :, :].rearrange("g p j -> (g p) j")).then_inc(idx_in[s], 16)
            for turn in range(TURNS):
                sp.wait_ge(out_ready, turn + 1)
                full = Q if turn < TURNS - 1 else Q - 1
                t0 = turn * Q
                sp.dma_start(nodes(out[t0 * P:(t0 + full) * P, :]), xc[:, t0:t0 + full, :]).then_inc(out_written, 16)
            sp.dma_start(out[(TILES - 1) * P:N, :], xc[0:LAST, TILES - 1, :]).then_inc(out_written, 16)
            sp.wait_ge(out_written, 16 * (TURNS + 1))

        @block.gpsimd
        def _(pool):
            pool.iota(iota[:, :], [[1, W]], base=0, channel_multiplier=0,
                      allow_small_or_imprecise_dtypes=True).then_inc(pool_consts, 1)
            pool.iota(shifts[:, :], [[W, WMAX]], base=0, channel_multiplier=0,
                      allow_small_or_imprecise_dtypes=True).then_inc(pool_consts, 1)
            pool.memset(ident[:, :], 0.0).then_inc(pool_consts, 1)
            pool.wait_ge(pool_consts, 3)
            pool.affine_select(out=ident[:, :], in_=ident[:, :], compare_op=ALU.not_equal, fill=1.0, base=0,
                               pattern=[[-1, P]], channel_multiplier=1).then_inc(pool_consts, 1)
            for n in range(2):
                pool.memset(acc[n][:, :], 0.0).then_inc(acc_ready, 1)
            for layer, gat, used in ((0, gat0, msg_done), (1, gat1, agg_done)):
                pool.wait_ge(table_out, 16 * (layer + 1))
                with pool.Fori(0, STEPS) as it:
                    for s in range(S):
                        pool.wait_ge(used[s], after(it, layer * STEPS - 1))
                        pool.nop(nofuse=True)
                        pool.wait_ge(idx_in[s], it * 16 + (16 * layer * STEPS + 16))
                        pool.nop(nofuse=True)
                        for j in range(J):
                            pool.indirect_dma_start(gat[s][:, j, :], None, table[layer],
                                                    bass.IndirectOffsetOnAxis(ap=idx[s][:, j:j + 1], axis=0)).then_inc(gat_in[s], 16)

        @block.scalar
        def _(act):
            def root_of(n):
                act.wait_ge(var_ready, n + 1)
                nc.scalar.activation(stat[:, 2, :], stat[:, 1, :], ACT.Sqrt).then_inc(std_ready, 1)

            def relu(it, s):
                for half in range(2):
                    act.wait_ge(hid_done[half][s], after(it))
                    if half == 0:
                        act.wait_ge(w_done[(s - 1) % S], after(it, -1 if s == 0 else 0))
                    cols = slice(half * HALF, (half + 1) * HALF)
                    nc.scalar.activation(hid[0:D, cols], hid_ps[0:D, cols], ACT.Relu, bias=b1_sb[:, :]).then_inc(relu_done[half][s], 1)

            def split(it, s):
                parts = parts0[s % 2]
                act.wait_ge(msg_done[s], after(it))
                act.wait_ge(agg_done[(s - 2) % S], after(it, -1 if s < 2 else 0))
                nc.scalar.activation(parts[:, :, 0, :], msg[:, :, :], ACT.Copy).then_inc(part1_done[s], 1)
                act.wait_ge(rest_done[s], after(it))
                nc.scalar.activation(parts[:, :, 1, :], rest[:, :, :], ACT.Copy).then_inc(part2_done[s], 1)

            root_of(0)
            act.wait_ge(h_ready, 1)
            with act.Fori(0, TURNS) as it:
                act.wait_ge(trans_done, it + 1)
                nc.scalar.activation(stage, h_sb[:, bass.ds(it * Q, Q), :], ACT.Copy).then_inc(stage_done, 1)
                act.wait_ge(trans_done, it + 2)
                act.wait_ge(node_done, it + 1)
                nc.scalar.activation(at, at_ps[0:D1, 0:Q, :], ACT.Copy).then_inc(copied, 1)

            act.wait_ge(weights_in, 160)
            act.wait_ge(dve_consts, 1)
            relu(0, 0)
            with act.Fori(0, STEPS - 1) as it:
                for s in range(S):
                    relu(it + (s + 1) // S, (s + 1) % S)
                    split(it, s)
            for s in range(S):
                if s < S - 1:
                    relu(STEPS - 1, s + 1)
                split(STEPS - 1, s)

            def sums(layer):
                act.wait_ge(added[S - 1], after(STEPS * (layer + 1) - 1))
                with act.Fori(0, TURNS) as it:
                    act.wait_ge(node_done, it + (TURNS * (layer + 1) + 1))
                    nc.scalar.activation(at, acc[layer][:, bass.ds(it * (Q * P), Q * P)].rearrange("p (q n) -> p q n", n=P),
                                         ACT.Copy).then_inc(copied, 1)

            sums(0)
            root_of(1)
            act.wait_ge(h_ready, 2)
            nc.scalar.activation(parts1[:, :, 0, 0:D], h_sb[:, :, 0:D], ACT.Copy).then_inc(table_parts, 1)
            act.wait_ge(table_parts, 2)
            nc.scalar.activation(parts1[:, :, 1, 0:D], xc[:, :, :], ACT.Copy).then_inc(table_parts, 1)
            sums(1)

        @block.tensor
        def _(pe):
            pe.sem_inc(trans_done, 1)
            pe.sem_inc(node_done, 1)
            pe.wait_ge(weights_in, 160)
            pe.wait_ge(pool_consts, 4)
            pe.wait_ge(bounds_in, 16)
            pe.wait_ge(dve_consts, 2)
            windows = pe.alloc_register("pe_windows")
            pe.reg_mov(windows, 0)

            def window_sum(to, parts, width, hot):
                for j in range(J):
                    for r in range(R):
                        last = nc.tensor.matmul(to[0:width, 0:W], parts[:, j, r, 0:width], hot[:, j, :],
                                                start=(j == 0 and r == 0), stop=(j == J - 1 and r == R - 1))
                return last

            def aggregate(it, s, turn, parts, width):
                g = it * S + s
                more = pe.value_load(bounds[0:1, bass.ds(g + 2 * GROUPS, 1)], min_val=0, max_val=1)
                with pe.If(more > 0):
                    base = pe.value_load(bounds[0:1, bass.ds(g, 1)], min_val=0, max_val=NPAD - 1)
                    end = pe.value_load(bounds[0:1, bass.ds(g + GROUPS, 1)], min_val=1, max_val=NPAD)
                    with pe.Fori(base + W, end, W) as _at:
                        n = pe.snap(windows)
                        pe.wait_ge(x_onehot_done, n + 1)
                        window_sum(node_ps[:, 0, :], parts, width, x_onehot).then_inc(x_agg_done, 1)
                        pe.reg_add(windows, windows, 1)
                pe.wait_ge(onehot_done[s], after(turn))
                pe.wait_ge(added[(s - 2) % S], after(turn, -1 if s < 2 else 0))
                window_sum(agg_ps[s % 2], parts, width, onehot[s % 2]).then_inc(agg_done[s], 1)

            def hidden(it, s):
                pe.wait_ge(ea_in[s], it * 16 + 16)
                for half in range(2):
                    pe.wait_ge(relu_done[half][(s - 1) % S], after(it, -1 if s == 0 else 0))
                    cols = slice(half * HALF, (half + 1) * HALF)
                    nc.tensor.matmul(hid_ps[0:D, cols], w1t_sb[:, :], ea[s][:, cols], start=True, stop=True).then_inc(hid_done[half][s], 1)

            def edge_weights(it, s):
                pe.wait_ge(msg_done[(s - 1) % S], after(it, -1 if s == 0 else 0))
                for half in range(2):
                    pe.wait_ge(relu_done[half][s], after(it))
                    for j in range(half * J // 2, (half + 1) * J // 2):
                        last = nc.tensor.matmul(w_ps[:, j, 0:D], hid[:, j * P:(j + 1) * P], w2t_sb[:, :], start=True, stop=True)
                last.then_inc(w_done[s], 1)

            def node_products(it, before, weights, rows, cols):
                pe.wait_ge(copied, it + (before + 1))
                pe.wait_ge(node_used, it + (before + 1))
                for q in range(Q):
                    last = nc.tensor.matmul(node_ps[:, q, 0:cols], at[0:rows, q, :], weights[0:rows, 0:cols], start=True, stop=True)
                last.then_inc(node_done, 1)

            with pe.Fori(0, TURNS) as it:
                pe.wait_ge(stage_done, it + 1)
                for q in range(Q):
                    last = nc.tensor.transpose(at_ps[0:D1, q, :], stage[:, q, :], ident[:, :])
                last.then_inc(trans_done, 1)
                node_products(it, 0, wst_sb, D1, D)

            def group0(it, s, ahead=2):
                if ahead >= 1:
                    edge_weights(it + (s + 1) // S, (s + 1) % S)
                if ahead >= 2:
                    hidden(it + (s + 2) // S, (s + 2) % S)
                pe.wait_ge(part2_done[s], after(it))
                pe.wait_ge(part3_done[s], after(it))
                aggregate(it, s, it, parts0[s % 2][:, :, :, :], D)

            hidden(0, 0)
            edge_weights(0, 0)
            hidden(0, 1)
            with pe.Fori(0, STEPS - 1) as it:
                for s in range(S):
                    group0(it, s)
            for s in range(S):
                group0(STEPS - 1, s, ahead=min(2, S - 1 - s))

            with pe.Fori(0, TURNS) as it:
                node_products(it, TURNS, wnt_sb, D, D)

            with pe.Fori(0, STEPS) as it:
                for s in range(S):
                    pe.wait_ge(gat_in[s], it * (16 * J) + (16 * J * (STEPS + 1)))
                    aggregate(it, s, it + STEPS, gat1[s][:, :, 0:R * D1].rearrange("p j (r d) -> p j r d", r=R), D1)

            with pe.Fori(0, TURNS) as it:
                node_products(it, 2 * TURNS, w_sb, D1, D1)

        @block.vector
        def _(dve):
            steps = [0]

            def step(ins):
                steps[0] += 1
                ins.then_inc(dve_step, 1)
                dve.wait_ge(dve_step, steps[0])

            def per_tile(a):
                return a.unsqueeze(2).to_broadcast([P, TILES, D])

            def layernorm(n):
                step(nc.vector.reduce_sum(stat[:, 0, :], x_sb[:, :, :], axis=AX.X))
                step(nc.vector.tensor_single_scalar(stat[:, 0, :], stat[:, 0, :], 1.0 / D, ALU.mult))
                step(nc.vector.tensor_tensor(xc[:, :, :], x_sb[:, :, :], per_tile(stat[:, 0, :]), ALU.subtract))
                step(nc.vector.tensor_tensor(h_sb[:, :, 0:D], xc[:, :, :], xc[:, :, :], ALU.mult))
                step(nc.vector.reduce_sum(stat[:, 1, :], h_sb[:, :, 0:D], axis=AX.X))
                nc.vector.tensor_scalar(stat[:, 1, :], stat[:, 1, :], 1.0 / D, EPS, ALU.mult, ALU.add).then_inc(var_ready, 1)
                dve.wait_ge(std_ready, n + 1)
                step(nc.vector.reciprocal(stat[:, 3, :], stat[:, 2, :]))
                nc.vector.scalar_tensor_tensor(h_sb[:, :, 0:D], xc[:, :, :], 0.0, per_tile(stat[:, 3, :]), ALU.max, ALU.mult).then_inc(h_ready, 1)

            nc.vector.memset(x_sb[:, TILES - 1, :], 0.0).then_inc(x_zeroed, 1)
            nc.vector.memset(hid[D:D1, :], 1.0).then_inc(dve_consts, 1)
            nc.vector.memset(h_sb[:, :, D:D1], 1.0)
            nc.vector.memset(w_sb[:, D:D1], 0.0).then_inc(dve_step, 1)
            steps[0] += 1
            dve.wait_ge(dve_step, steps[0])
            step(nc.vector.memset(w_sb[D:D1, D:D1], 1.0))
            dve.wait_ge(dstb_in, 16)
            step(nc.vector.tensor_reduce(bnd[:, 0, :], dst_b, axis=AX.X, op=ALU.min))
            step(nc.vector.tensor_reduce(bnd[:, 1, :], dst_b, axis=AX.X, op=ALU.max))
            step(nc.vector.tensor_single_scalar(bnd[:, 1, :], bnd[:, 1, :], 1, ALU.add))
            step(nc.vector.tensor_tensor(bnd[:, 2, :], bnd[:, 1, :], bnd[:, 0, :], ALU.subtract))
            nc.vector.tensor_single_scalar(bnd[:, 2, :], bnd[:, 2, :], W, ALU.is_gt).then_inc(bounds_ready, 1)
            dve.wait_ge(bounds_ready, 1)
            step(nc.vector.memset(parts1_rows[:, :, :], 0.0))
            step(nc.vector.memset(parts1[:, :, 0, D:D1], 1.0))
            dve.wait_ge(dst_in, 16)
            step(nc.vector.tensor_copy(rel[:, :, :], dst_i.rearrange("p (g j) -> p g j", j=J)))
            dve.wait_ge(weights_in, 160)
            nc.vector.tensor_tensor(wst_sb[D:D1, :], wst_sb[D:D1, :], wnt_sb[D:D1, :], ALU.add).then_inc(dve_consts, 1)
            dve.wait_ge(x_in, 32)
            layernorm(0)
            dve.wait_ge(base_in, 16)
            step(nc.vector.tensor_copy(base_f[:, :], base_i[:, :]))
            step(nc.vector.tensor_tensor(rel[:, :, :], rel[:, :, :], base_f[:, :].unsqueeze(2).to_broadcast([P, GROUPS, J]), ALU.subtract))

            dve.sem_inc(node_used, 1)
            with dve.Fori(0, TURNS) as it:
                dve.wait_ge(node_done, it + 2)
                nc.vector.tensor_copy(root[:, bass.ds(it * Q, Q), :], node_ps[:, 0:Q, 0:D]).then_inc(node_used, 1)

            dve.wait_ge(bounds_in, 16)
            dve.wait_ge(pool_consts, 4)
            dve.wait_ge(acc_ready, 2)
            windows = dve.alloc_register("dve_windows")
            dve.reg_mov(windows, 0)
            base_before = dve.alloc_register("base_before")
            dve.sem_inc(x_added, 1)
            window = dve.alloc_register("window")

            def compare(to, numbers):
                return nc.vector.tensor_tensor(to[:, :, :], iota[:, :].unsqueeze(1).to_broadcast([P, J, W]),
                                               numbers.unsqueeze(2).to_broadcast([P, J, W]), ALU.is_equal)

            def add_before(turn, s, layer, width):
                b = (s - 1) % S
                wraps = -1 if s == 0 else 0
                base = dve.snap(base_before, min_val=0, max_val=NPAD - 1)
                dve.wait_ge(agg_done[b], after(turn, wraps))
                dve.wait_ge(added[(s - 2) % S], after(turn, -1 if s < 2 else 0))
                to = acc[layer][0:width, bass.ds(base, W)]
                nc.vector.tensor_tensor(to, to, agg_ps[b % 2][0:width, 0:W], ALU.add).then_inc(added[b], 1)

            def further_windows(g, base, layer, width):
                more = dve.value_load(bounds[0:1, bass.ds(g + 2 * GROUPS, 1)], min_val=0, max_val=1)
                with dve.If(more > 0):
                    end = dve.value_load(bounds[0:1, bass.ds(g + GROUPS, 1)], min_val=1, max_val=NPAD)
                    dve.reg_mov(window, 1)
                    with dve.Fori(base + W, end, W) as at_node:
                        n = dve.snap(windows)
                        k = dve.snap(window, min_val=1, max_val=WMAX - 1)
                        nc.vector.tensor_scalar(x_rel[:, :], rel[:, bass.ds(g, 1), :].rearrange("p g j -> p (g j)"),
                                                shifts[:, bass.ds(k, 1)], None, ALU.subtract).then_inc(x_rel_done, 1)
                        dve.wait_ge(x_rel_done, n + 1)
                        compare(x_onehot, x_rel[:, :]).then_inc(x_onehot_done, 1)
                        dve.wait_ge(x_agg_done, n + 1)
                        dve.wait_ge(x_added, n + 1)
                        to = acc[layer][0:width, bass.ds(at_node, W)]
                        nc.vector.tensor_tensor(to, to, node_ps[0:width, 0, 0:W], ALU.add).then_inc(x_added, 1)
                        dve.reg_add(windows, windows, 1)
                        dve.reg_add(window, window, 1)
                    n = dve.snap(windows)
                    dve.wait_ge(x_added, n + 1)
                    dve.nop(nofuse=True)

            def group0(it, s, first=False):
                g = it * S + s
                base = dve.value_load(bounds[0:1, bass.ds(g, 1)], min_val=0, max_val=NPAD - 1)
                compare(onehot[s % 2], rel[:, bass.ds(g, 1), :].rearrange("p g j -> p (g j)")).then_inc(onehot_done[s], 1)
                dve.wait_ge(gat_in[s], it * (16 * J) + 16 * J)
                dve.wait_ge(w_done[s], after(it))
                nc.vector.tensor_tensor(msg[:, :, :], w_ps[:, :, 0:D], gat0[s], ALU.mult).then_inc(msg_done[s], 1)
                if not first:
                    add_before(it, s, 0, D)
                dve.reg_mov(base_before, base)
                dve.wait_ge(part1_done[s], after(it))
                nc.vector.tensor_tensor(rest[:, :, :], msg[:, :, :], parts0[s % 2][:, :, 0, :], ALU.subtract).then_inc(rest_done[s], 1)
                dve.wait_ge(part2_done[s], after(it))
                nc.vector.tensor_tensor(parts0[s % 2][:, :, 2, :], rest[:, :, :], parts0[s % 2][:, :, 1, :], ALU.subtract).then_inc(part3_done[s], 1)
                further_windows(g, base, 0, D)

            def group1(it, s, first=False):
                g = it * S + s
                base = dve.value_load(bounds[0:1, bass.ds(g, 1)], min_val=0, max_val=NPAD - 1)
                compare(onehot[s % 2], rel[:, bass.ds(g, 1), :].rearrange("p g j -> p (g j)")).then_inc(onehot_done[s], 1)
                if not first:
                    add_before(it + STEPS, s, 1, D1)
                dve.reg_mov(base_before, base)
                further_windows(g, base, 1, D1)

            for s in range(S):
                group0(0, s, first=(s == 0))
            with dve.Fori(1, STEPS) as it:
                for s in range(S):
                    group0(it, s)
            add_before(STEPS, 0, 0, D)

            with dve.Fori(0, TURNS) as it:
                tiles = x_sb[:, bass.ds(it * Q, Q), :]
                r = root[:, bass.ds(it * Q, Q), :]
                dve.wait_ge(node_done, it + (TURNS + 2))
                nc.vector.tensor_tensor(r, node_ps[:, 0:Q, 0:D], r, ALU.add).then_inc(node_used, 1)
                dve.wait_ge(node_used, it + (TURNS + 2))
                nc.vector.scalar_tensor_tensor(tiles, r, 0.0, tiles, ALU.max, ALU.add).then_inc(x_updated, 1)
            dve.wait_ge(x_updated, TURNS)
            layernorm(1)
            dve.wait_ge(table_parts, 1)
            nc.vector.tensor_tensor(xc[:, :, :], h_sb[:, :, 0:D], parts1[:, :, 0, 0:D], ALU.subtract).then_inc(table_parts, 1)
            dve.wait_ge(table_parts, 3)
            nc.vector.tensor_tensor(parts1[:, :, 2, 0:D], xc[:, :, :], parts1[:, :, 1, 0:D], ALU.subtract).then_inc(table_ready, 1)

            for s in range(S):
                group1(0, s, first=(s == 0))
            with dve.Fori(1, STEPS) as it:
                for s in range(S):
                    group1(it, s)
            add_before(2 * STEPS, 0, 1, D1)

            with dve.Fori(0, TURNS) as it:
                o = xc[:, bass.ds(it * Q, Q), :]
                deg = stat[:, 0, 0:Q]
                inv = stat[:, 1, 0:Q]
                dve.wait_ge(node_done, it + (2 * TURNS + 2))
                nc.vector.tensor_single_scalar(deg, node_ps[:, 0:Q, D], 1.0, ALU.max).then_inc(scaled, 1)
                dve.wait_ge(scaled, it * 3 + 1)
                nc.vector.reciprocal(inv, deg).then_inc(scaled, 1)
                dve.wait_ge(scaled, it * 3 + 2)
                nc.vector.tensor_tensor(o, node_ps[:, 0:Q, 0:D], inv.unsqueeze(2).to_broadcast([P, Q, D]), ALU.mult).then_inc(scaled, 1)
                dve.wait_ge(scaled, it * 3 + 3)
                dve.sem_inc(node_used, 1)
                nc.vector.tensor_tensor(o, o, x_sb[:, bass.ds(it * Q, Q), :], ALU.add).then_inc(out_ready, 1)


def kernel(x, src, dst, edge_attr_17, L0_gnn_W1, L0_gnn_b1, L0_gnn_W2, L0_gnn_b2, L0_gnn_Ws, L0_gnn_bs,
           L0_gnn_Wn, L0_gnn_bn, L1_gnn_W, L1_gnn_b):
    import numpy as np
    import concourse.bacc as bacc
    from concourse.bass_utils import run_bass_kernel_spmd

    def padded(a, fill):
        return np.concatenate([np.asarray(a), np.full((EPAD - E, *a.shape[1:]), fill, np.asarray(a).dtype)])

    src_p = padded(src, 0).reshape(GROUPS, J, P)
    dst_p = padded(dst, NPAD - 1)
    ea_p = padded(edge_attr_17, 0).reshape(GROUPS, GE, DE)
    arrays = {
        "x": x,
        "src_ids": src_p.transpose(0, 2, 1),
        "dst_ids": dst_p.reshape(GROUPS * J, P).T,
        "dst_flat": dst_p,
        "edge_attr": ea_p.transpose(0, 2, 1),
        "w1t": np.asarray(L0_gnn_W1).T, "b1": np.asarray(L0_gnn_b1).reshape(D, 1),
        "w2t": np.asarray(L0_gnn_W2).T, "b2": np.asarray(L0_gnn_b2).reshape(1, D),
        "wst": np.asarray(L0_gnn_Ws).T, "bs": np.asarray(L0_gnn_bs).reshape(1, D),
        "wnt": np.asarray(L0_gnn_Wn).T, "bn": np.asarray(L0_gnn_bn).reshape(1, D),
        "w": L1_gnn_W, "b": np.asarray(L1_gnn_b).reshape(1, D),
    }
    nc = bacc.Bacc("TRN2", target_bir_lowering=False, num_devices=1)
    arrays = {k: np.ascontiguousarray(v) for k, v in arrays.items()}
    aps = [nc.dram_tensor(k, v.shape, mybir.dt.from_np(v.dtype), kind="ExternalInput").ap() for k, v in arrays.items()]
    out = nc.dram_tensor("out", (N, D), F32, kind="ExternalOutput").ap()
    gnn_program(nc, *aps, out)
    return run_bass_kernel_spmd(nc, [arrays], core_ids=[0]).results[0]["out"]
```

```python
from contextlib import ExitStack

import concourse.bass as bass
from concourse import mybir

F32 = mybir.dt.float32
BF16 = mybir.dt.bfloat16
F16 = mybir.dt.float16
I32 = mybir.dt.int32
ALU = mybir.AluOpType
ACT = mybir.ActivationFunctionType
AX = mybir.AxisListType

P = 128
N = 6250
E = 200000
D = 96
DE = 17
D1 = D + 1
R = 3
PW = R * D1 + 1
TILES = -(-N // P)
LAST = N - (TILES - 1) * P
NPAD = TILES * P
Q = 7
TURNS = TILES // Q
J = 8
GE = J * P
GROUPS = -(-E // GE)
EPAD = GROUPS * GE
S = 4
STEPS = GROUPS // S
W = 96
WMAX = -(-NPAD // W)
HALF = 512
BP = 98
BQ = GROUPS // BP
EPS = 1e-5

BANKS = 4
HOTS = 3
U = 2


class Section:

    def __init__(self, before, group0, turns, groups, units, parts, nodes):
        self.turns, self.groups, self.units, self.parts, self.nodes = turns, groups, units, parts, nodes
        self.window = parts * nodes
        self.keys = TILES * nodes
        self.tiles = J // units
        self.fills = groups * units * parts
        self.adds = groups * units
        self.turn0 = before.turn_end if before else 0
        self.group0 = group0
        self.order0 = before.order0 + before.turns * before.groups if before else 0
        self.fill0 = before.fill0 + before.turns * before.fills if before else 0
        self.add0 = before.add0 + before.turns * before.adds if before else 0
        self.turn_end = self.turn0 + turns
        self.group_end = self.group0 + turns * groups

    def group(self, t, c):
        return t * self.groups + (self.group0 - self.turn0 * self.groups + c)

    def order(self, t, c):
        return t * self.groups + (self.order0 - self.turn0 * self.groups + c)

    def fill(self, t, n):
        return t * self.fills + (self.fill0 - self.turn0 * self.fills + n)

    def add(self, t, n):
        return t * self.adds + (self.add0 - self.turn0 * self.adds + n)


def sections(*shapes):
    made = []
    for shape in shapes:
        made.append(Section(made[-1] if made else None, *shape))
    return made


SECTIONS = sections((0, 2, 8, 1, 1, 10), (24, 3, 8, 2, 1, 10), (48, 3, 6, 2, 2, 7), (66, 3, 6, 2, 2, 8), (84, 5, 4, 2, 2, 10),
                    (104, 3, 4, 2, 3, 8), (16, 1, 8, 1, 1, 10))
TURNS1 = SECTIONS[-1].turn_end
CG = max(x.group_end for x in SECTIONS)
SKIP = CG // S
KEYS = max(x.keys for x in SECTIONS)
LOWS = P * max(x.parts for x in SECTIONS)
assert sum(x.turns * x.groups for x in SECTIONS) == CG == SKIP * S and SKIP + TURNS1 == STEPS
assert all(x.fills % BANKS == 0 and x.adds % 4 == 0 and x.groups % 2 == 0 and x.keys <= HALF and x.adds * x.window <= HALF for x in SECTIONS)
assert GROUPS % S == 0 and TILES % Q == 0 and GROUPS % BP == 0


def after(it, wraps=0):
    return it + (2 + wraps)


def gnn_program(nc, x, src_ids, src_cols, dst_ids, dst_flat, edge_attr, w1t, b1, w2t, b2, wst, bs, wnt, bn, w, b, out):
    table = [nc.dram_tensor("node_table0", (NPAD, D), F32, kind="Internal").ap(),
             nc.dram_tensor("node_table1", (NPAD, PW), BF16, kind="Internal").ap()]
    bounds_dram = nc.dram_tensor("bounds_dram", (3, GROUPS), I32, kind="Internal").ap()

    units_dram = nc.dram_tensor("units_dram", (2, U * GROUPS), I32, kind="Internal").ap()

    with ExitStack() as ctx:
        def sb(name, shape, dt=F32):
            return ctx.enter_context(nc.sbuf_tensor(name, shape, dt))

        def sem(name):
            return ctx.enter_context(nc.semaphore(name))

        def slots(name):
            return [sem(f"{name}{s}") for s in range(S)]

        x_sb = sb("x_sb", [P, TILES, D])
        xc = sb("xc", [P, TILES, D])
        h_sb = sb("h_sb", [P, TILES, D1])
        parts1_rows = sb("parts1_rows", [P, TILES, PW], BF16)
        parts1 = parts1_rows[:, :, 0:R * D1].rearrange("p t (r d) -> p t r d", r=R)
        root = xc
        stat = sb("stat", [P, 4, TILES])
        acc = [sb(f"acc{n}", [D1, NPAD + W]) for n in range(2)]
        rel = sb("rel", [P, GROUPS, J])
        base_f = sb("base_f", [P, GROUPS])
        bnd = sb("bnd", [BP, 3, BQ], I32)
        bnd_units = sb("bnd_units", [BP, 2, U * BQ], I32)
        bounds = sb("bounds", [1, 3 * GROUPS], I32)
        unit_bounds = sb("unit_bounds", [1, 2 * U * CG], I32)
        parts1_flat = parts1_rows[:, :, :].rearrange("p t d -> p (t d)")
        dst_i = parts1_flat[:, 2 * BQ * GE:2 * BQ * GE + 2 * GROUPS * J].bitcast(I32)
        dst_b = parts1_flat[0:BP, 0:2 * BQ * GE].bitcast(I32)\
            .rearrange("p (q e) -> p q e", e=GE)
        iota = sb("iota", [P, W])
        ident = sb("ident", [P, P])
        idx = [sb(f"idx{s}", [P, J], I32) for s in range(S)]
        gat1 = [sb(f"gat{s}", [P, J, PW], BF16) for s in range(S)]
        gat0 = [t[:, :, :].rearrange("p j d -> p (j d)")[:, 0:2 * J * D].bitcast(F32).rearrange("p (j d) -> p j d", d=D)
                for t in gat1]
        arena = sb("arena", [P, S * GE + GE + 2 * J * D])
        ea = [arena[0:DE, s * GE:(s + 1) * GE] for s in range(S)]
        hid = arena[0:D1, S * GE:(S + 1) * GE]
        msg, rest = [arena[:, (S + 1) * GE + u * J * D:(S + 1) * GE + (u + 1) * J * D].rearrange("p (j d) -> p j d", d=D)
                     for u in range(2)]
        parts0 = [sb(f"parts0_{u}", [P, J, R, D], BF16) for u in range(2)]
        onehot = [sb(f"onehot{u}", [P, J, W], BF16) for u in range(2)]
        base_i = onehot[1][:, :, :].rearrange("p j n -> p (j n)")[:, 0:2 * GROUPS].bitcast(I32)
        x_rel = sb("x_rel", [P, J])
        x_onehot = sb("x_onehot", [P, J, W], BF16)
        stage = parts0[0][:, :, :, :].rearrange("p j r d -> p (j r d)")[:, 0:2 * Q * D1].bitcast(F32)\
            .rearrange("p (q d) -> p q d", d=D1)
        shifts = sb("shifts", [P, WMAX])
        at = parts0[1][0:D1, :, :, :].rearrange("p j r d -> p (j r d)")[:, 0:2 * Q * P].bitcast(F32)\
            .rearrange("p (q n) -> p q n", n=P)
        iota16 = sb("iota16", [P, HALF], F16)
        num_now = [sb(f"num_now{u}", [P, 2, J]) for u in range(2)]
        bad = sb("bad", [1, 8], I32)
        wide_f = sb("wide_f", [1, 8])
        spans = x_onehot[0:1, :, :].rearrange("p j n -> p (j n)")[:, 0:2 * U * CG].bitcast(F32)
        arena16 = arena[:, :].bitcast(F16)
        xc_flat = xc[:, :, :].rearrange("p t d -> p (t d)")
        parts16 = [t[:, :, :, :].rearrange("p j r d -> p (j r d)").bitcast(F16) for t in parts0]
        xc16 = xc_flat.bitcast(F16)
        low0, low1 = 2 * J * KEYS, 4 * CG * J

        def key_hot(b, tile, keys):
            room, start = (arena16, (b * J + tile) * KEYS) if b < 2 else (parts16[2 * tile // J], tile % (J // 2) * KEYS)
            return room[:, start:start + keys]

        def low_hot(b, tile, first, last):
            n = tile if b < 2 else J + tile % (J // 2)
            room, start = (arena16, low0) if b == 0 or (b == 2 and tile < J // 2) else (xc16, low1)
            return room[:, start + n * LOWS + first:start + n * LOWS + last]

        numbers = xc_flat[:, 0:2 * CG * J].rearrange("p (g c j) -> p g c j", c=2, j=J)
        work = [xc_flat[:, (2 + k) * CG * J:(3 + k) * CG * J].rearrange("p (g j) -> p g j", j=J) for k in range(3)]
        src_i = parts0[0][:, :, :, :].rearrange("p j r d -> p (j r d)")[:, 0:2 * CG * J].bitcast(I32)\
            .rearrange("p (g j) -> p g j", j=J)
        unit_i, unit_f = [onehot[u][:, :, :].rearrange("p j n -> p (j n)")[:, 0:2 * U * CG].bitcast(dt)
                          for u, dt in enumerate((I32, F32))]
        h16 = h_sb[:, :, :].rearrange("p t d -> p (t d)").bitcast(F16)

        def counts(x):
            return h16[:, 0:TILES * x.adds * x.window].rearrange("p (t w n) -> p t w n", w=x.adds, n=x.window)

        at2 = [at, parts0[0][0:D1, :, :, :].rearrange("p j r d -> p (j r d)")[:, 0:2 * Q * P].bitcast(F32)
               .rearrange("p (q n) -> p q n", n=P)]
        w1t_sb = sb("w1t_sb", [DE, D])
        b1_sb = sb("b1_sb", [D, 1])
        w2t_sb = sb("w2t_sb", [D1, D])
        wst_sb = sb("wst_sb", [D1, D])
        wnt_sb = sb("wnt_sb", [D1, D])
        w_sb = sb("w_sb", [D1, D1])

        hid_ps = ctx.enter_context(nc.psum_tensor("hid_ps", [P, 2 * HALF], F32))
        w_ps = ctx.enter_context(nc.psum_tensor("w_ps", [P, J, P], F32))
        agg_ps = [ctx.enter_context(nc.psum_tensor(f"agg_ps{u}", [P, HALF], F32)) for u in range(2)]
        node_ps = ctx.enter_context(nc.psum_tensor("node_ps", [P, J, P], F32))
        trans_ps = [w_ps, hid_ps[:, :].rearrange("p (j n) -> p j n", n=P)]
        node2_ps = [node_ps, w_ps]
        w_flat = w_ps[:, :, :].rearrange("p j n -> p (j n)")
        count_ps = [bank[:, half * HALF:(half + 1) * HALF] for bank in (hid_ps[:, :], w_flat) for half in range(2)]
        applied_ps = node_ps[:, :, :].rearrange("p j n -> p (j n)")[:, HALF:2 * HALF]

        x_zeroed = sem("x_zeroed")
        x_in = [sem(f"x_in{turn}") for turn in range(TURNS)]
        dst_in = sem("dst_in")
        dstb_in = sem("dstb_in")
        weights_in = sem("weights_in")
        bounds_ready = sem("bounds_ready")
        bounds_out = sem("bounds_out")
        bounds_in = sem("bounds_in")
        base_in = sem("base_in")
        pool_consts = sem("pool_consts")
        dve_consts = sem("dve_consts")
        dve_step = sem("dve_step")
        var_ready = sem("var_ready")
        std_ready = sem("std_ready")
        mean_step = sem("mean_step")
        centered = sem("centered")
        squared = sem("squared")
        summed = sem("summed")
        normal_done = sem("normal_done")
        first_part = sem("first_part")
        rest_ready = sem("rest_ready")
        second_part = sem("second_part")
        table_ready = sem("table_ready")
        table_out = sem("table_out")
        acc_ready = sem("acc_ready")
        idx_in = slots("idx_in")
        ea_in = slots("ea_in")
        gat_in = [slots("gat0_in"), slots("gat1_in")]
        hid_done = [slots("hid_done_a"), slots("hid_done_b")]
        relu_done = [slots("relu_done_a"), slots("relu_done_b")]
        w_done = slots("w_done")
        msg_done = slots("msg_done")
        part1_done = slots("part1_done")
        rest_done = slots("rest_done")
        part2_done = slots("part2_done")
        part3_done = slots("part3_done")
        onehot_done = slots("onehot_done")
        agg_done = slots("agg_done")
        added = slots("added")
        x_rel_done = sem("x_rel_done")
        x_onehot_done = sem("x_onehot_done")
        x_agg_done = sem("x_agg_done")
        x_added = sem("x_added")
        bad_ready = sem("bad_ready")
        units_ready = sem("units_ready")
        units_out = sem("units_out")
        units_in = sem("units_in")
        unit_in = sem("unit_in")
        src_in = sem("src_in")
        sums_ready = sem("sums_ready")
        num_copied = sem("num_copied")
        hot_ready = sem("hot_ready")
        counted = sem("counted")
        count_copied = sem("count_copied")
        applied = sem("applied")
        count_added = sem("count_added")
        stage_done = sem("stage_done")
        trans_done = sem("trans_done")
        copied = sem("copied")
        node_done = sem("node_done")
        node_used = sem("node_used")
        x_updated = sem("x_updated")
        scaled = sem("scaled")
        out_ready = sem("out_ready")
        out_written = sem("out_written")

        block = ctx.enter_context(nc.Block())

        def nodes(t):
            return t.rearrange("(t p) d -> p t d", p=P)

        @block.sync
        def _(sp):
            sp.dma_start(dst_b, dst_flat.rearrange("(p q e) -> p q e", p=BP, e=GE)).then_inc(dstb_in, 16)
            sp.wait_ge(x_zeroed, 1)
            for turn in range(TURNS):
                t0, t1 = turn * Q, min((turn + 1) * Q, TILES - 1)
                sp.dma_start(x_sb[:, t0:t1, :], nodes(x[t0 * P:t1 * P, :])).then_inc(x_in[turn], 16)
            sp.dma_start(x_sb[0:LAST, TILES - 1, :], x[(TILES - 1) * P:N, :]).then_inc(x_in[TURNS - 1], 16)
            sp.dma_start(dst_i, dst_ids).then_inc(dst_in, 16)
            for tile, array in ((w1t_sb[:, :], w1t), (b1_sb[:, :], b1), (w2t_sb[0:D, :], w2t), (w2t_sb[D:D1, :], b2),
                                (wst_sb[0:D, :], wst), (wst_sb[D:D1, :], bs), (wnt_sb[0:D, :], wnt),
                                (wnt_sb[D:D1, :], bn), (w_sb[0:D, 0:D], w), (w_sb[D:D1, 0:D], b)):
                sp.dma_start(tile, array).then_inc(weights_in, 16)
            for group in (*hid_done, *relu_done, w_done, msg_done, part1_done, rest_done, part2_done, part3_done,
                          onehot_done, agg_done, added):
                for slot in group:
                    sp.sem_inc(slot, 1)
            for start in (*[count_copied] * BANKS, applied, count_added):
                sp.sem_inc(start, 1)
            sp.wait_ge(bounds_ready, 1)
            sp.dma_start(bounds_dram.rearrange("c (p q) -> p c q", p=BP), bnd[:, :, :]).then_inc(bounds_out, 16)
            sp.wait_ge(bounds_out, 16)
            sp.dma_start(bounds[:, :], bounds_dram.rearrange("c g -> (c g)").rearrange("(a n) -> a n", a=1)).then_inc(bounds_in, 16)
            sp.dma_start(base_i, bounds_dram[0:1, :].to_broadcast([P, GROUPS])).then_inc(base_in, 16)

            sp.dma_start(units_dram.rearrange("c (p q) -> p c q", p=BP), bnd_units[:, :, :]).then_inc(units_out, 16)
            sp.wait_ge(units_out, 16)
            sp.dma_start(unit_bounds[:, :].rearrange("a (c n) -> a c n", c=2),
                         units_dram[:, 0:U * CG].rearrange("(a c) n -> a c n", a=1)).then_inc(units_in, 16)

            with sp.Fori(0, TURNS) as it:
                sp.wait_ge(normal_done, it + 1)
                sp.dma_start(nodes(table[0][bass.ds(it * (Q * P), Q * P), :]), h_sb[:, bass.ds(it * Q, Q), 0:D]).then_inc(table_out, 16)
            with sp.Fori(0, STEPS) as it:
                for s in range(S):
                    g = it * S + s
                    sp.wait_ge(hid_done[1][s], after(it, -1))
                    sp.dma_start(ea[s][:, :], edge_attr[bass.ds(g, 1), :, :].rearrange("g c e -> (g c) e")).then_inc(ea_in[s], 16)
                    sp.wait_ge(msg_done[s], after(it, -1))
                    sp.dma_start(idx[s][:, :], src_ids[bass.ds(g, 1), :, :].rearrange("g p j -> (g p) j")).then_inc(idx_in[s], 16)
            for s in range(S):
                sp.wait_ge(agg_done[s], STEPS + 1)
            sp.dma_start(src_i, src_cols.rearrange("p (g j) -> p g j", j=J)).then_inc(src_in, 16)
            sp.dma_start(unit_i, units_dram[0:1, 0:U * CG].to_broadcast([P, U * CG])).then_inc(unit_in, 16)
            with sp.Fori(0, TURNS) as it:
                sp.wait_ge(table_ready, it + 1)
                sp.dma_start(nodes(table[1][bass.ds(it * (Q * P), Q * P), :]),
                             parts1_rows[:, bass.ds(it * Q, Q), :]).then_inc(table_out, 16)

            def second_ids(first):
                with sp.Fori(first, STEPS) as it:
                    for s in range(S):
                        g = it * S + s
                        sp.wait_ge(agg_done[s], after(it, STEPS - 1))
                        sp.dma_start(idx[s][:, :], src_ids[bass.ds(g, 1), :, :].rearrange("g p j -> (g p) j")).then_inc(idx_in[s], 16)

            sp.wait_ge(bad_ready, 1)
            wide = sp.value_load(bad[0:1, 0:1], min_val=0, max_val=8)
            with sp.If(wide > 0):
                second_ids(0)
            with sp.If(wide < 1):
                for s in range(S):
                    sp.sem_inc(idx_in[s], 16 * SKIP)
                second_ids(SKIP)
            for turn in range(TURNS):
                sp.wait_ge(out_ready, turn + 1)
                full = Q if turn < TURNS - 1 else Q - 1
                t0 = turn * Q
                sp.dma_start(nodes(out[t0 * P:(t0 + full) * P, :]), xc[:, t0:t0 + full, :]).then_inc(out_written, 16)
            sp.dma_start(out[(TILES - 1) * P:N, :], xc[0:LAST, TILES - 1, :]).then_inc(out_written, 16)
            sp.wait_ge(out_written, 16 * (TURNS + 1))

        @block.gpsimd
        def _(pool):
            pool.iota(iota[:, :], [[1, W]], base=0, channel_multiplier=0,
                      allow_small_or_imprecise_dtypes=True).then_inc(pool_consts, 1)
            pool.iota(shifts[:, :], [[W, WMAX]], base=0, channel_multiplier=0,
                      allow_small_or_imprecise_dtypes=True).then_inc(pool_consts, 1)
            pool.memset(ident[:, :], 0.0).then_inc(pool_consts, 1)
            pool.wait_ge(pool_consts, 3)
            pool.affine_select(out=ident[:, :], in_=ident[:, :], compare_op=ALU.not_equal, fill=1.0, base=0,
                               pattern=[[-1, P]], channel_multiplier=1).then_inc(pool_consts, 1)
            for n in range(2):
                pool.memset(acc[n][:, :], 0.0).then_inc(acc_ready, 1)
            pool.iota(iota16[:, :], [[1, HALF]], base=0, channel_multiplier=0,
                      allow_small_or_imprecise_dtypes=True).then_inc(pool_consts, 1)

            def squares(layer):
                with pool.Fori(0, TURNS) as it:
                    rows = h_sb[:, bass.ds(it * Q, Q), 0:D]
                    pool.wait_ge(centered, it + (layer * TURNS + 1))
                    pool.tensor_tensor(xc[:, bass.ds(it * Q, Q), :], rows, rows, ALU.mult).then_inc(squared, 1)

            def gathers(layer, gat, used, first):
                with pool.Fori(first, STEPS) as it:
                    for s in range(S):
                        pool.wait_ge(used[s], after(it, layer * STEPS - 1))
                        pool.nop(nofuse=True)
                        pool.wait_ge(idx_in[s], it * 16 + (16 * layer * STEPS + 16))
                        pool.nop(nofuse=True)
                        for j in range(J):
                            pool.indirect_dma_start(gat[s][:, j, :], None, table[layer],
                                                    bass.IndirectOffsetOnAxis(ap=idx[s][:, j:j + 1], axis=0)).then_inc(gat_in[layer][s], 16)

            squares(0)
            pool.wait_ge(table_out, 16 * TURNS)
            gathers(0, gat0, msg_done, 0)
            pool.wait_ge(bad_ready, 1)
            wide = pool.value_load(bad[0:1, 0:1], min_val=0, max_val=8)
            squares(1)
            with pool.Fori(0, TURNS) as it:
                pool.wait_ge(second_part, it + 1)
                pool.tensor_tensor(parts1[:, bass.ds(it * Q, Q), 2, 0:D], xc[:, bass.ds(it * Q, Q), :],
                                   parts1[:, bass.ds(it * Q, Q), 1, 0:D], ALU.subtract).then_inc(table_ready, 1)
            pool.wait_ge(table_out, 32 * TURNS)
            with pool.If(wide > 0):
                gathers(1, gat1, agg_done, 0)
            with pool.If(wide < 1):
                gathers(1, gat1, agg_done, SKIP)

        @block.scalar
        def _(act):
            def root_of(n, tiles):
                act.wait_ge(var_ready, n)
                nc.scalar.activation(stat[:, 2, tiles], stat[:, 1, tiles], ACT.Sqrt).then_inc(std_ready, 1)

            def relu(it, s):
                for half in range(2):
                    act.wait_ge(hid_done[half][s], after(it))
                    if half == 0:
                        act.wait_ge(w_done[(s - 1) % S], after(it, -1 if s == 0 else 0))
                    cols = slice(half * HALF, (half + 1) * HALF)
                    nc.scalar.activation(hid[0:D, cols], hid_ps[0:D, cols], ACT.Relu, bias=b1_sb[:, :]).then_inc(relu_done[half][s], 1)

            def split(it, s):
                parts = parts0[s % 2]
                act.wait_ge(msg_done[s], after(it))
                act.wait_ge(agg_done[(s - 2) % S], after(it, -1 if s < 2 else 0))
                nc.scalar.activation(parts[:, :, 0, :], msg[:, :, :], ACT.Copy).then_inc(part1_done[s], 1)
                act.wait_ge(rest_done[s], after(it))
                nc.scalar.activation(parts[:, :, 1, :], rest[:, :, :], ACT.Copy).then_inc(part2_done[s], 1)

            for turn in range(TURNS):
                root_of(turn + 1, slice(turn * Q, (turn + 1) * Q))

            def stage_of(it):
                act.wait_ge(normal_done, it + 1)
                act.wait_ge(trans_done, it + 1)
                nc.scalar.activation(stage, h_sb[:, bass.ds(it * Q, Q), :], ACT.Copy).then_inc(stage_done, 1)

            def transpose_of(it, u):
                act.wait_ge(trans_done, it + 2)
                act.wait_ge(node_done, it + 1)
                nc.scalar.activation(at, trans_ps[u][0:D1, 0:Q, :], ACT.Copy).then_inc(copied, 1)

            stage_of(0)
            with act.Fori(0, TURNS // 2) as pair:
                it = pair * 2
                for u in range(2):
                    stage_of(it + (u + 1))
                    transpose_of(it + u, u)
            transpose_of(TURNS - 1, 0)

            act.wait_ge(weights_in, 160)
            act.wait_ge(dve_consts, 1)
            relu(0, 0)
            with act.Fori(0, STEPS - 1) as it:
                for s in range(S):
                    relu(it + (s + 1) // S, (s + 1) % S)
                    split(it, s)
            for s in range(S):
                if s < S - 1:
                    relu(STEPS - 1, s + 1)
                split(STEPS - 1, s)

            def sums_of(layer, it):
                act.wait_ge(node_done, it + (TURNS * (layer + 1) + 1))
                nc.scalar.activation(at, acc[layer][:, bass.ds(it * (Q * P), Q * P)].rearrange("p (q n) -> p q n", n=P),
                                     ACT.Copy).then_inc(copied, 1)

            act.wait_ge(added[S - 1], after(STEPS - 1))
            def first_part_of(it):
                act.wait_ge(normal_done, it + (TURNS + 1))
                nc.scalar.activation(parts1[:, bass.ds(it * Q, Q), 0, 0:D], h_sb[:, bass.ds(it * Q, Q), 0:D],
                                     ACT.Copy).then_inc(first_part, 1)

            def second_part_of(it):
                act.wait_ge(rest_ready, it + 1)
                nc.scalar.activation(parts1[:, bass.ds(it * Q, Q), 1, 0:D], xc[:, bass.ds(it * Q, Q), :],
                                     ACT.Copy).then_inc(second_part, 1)

            with act.Fori(0, TURNS) as it:
                sums_of(0, it)
            root_of(TURNS + 1, slice(0, TILES))
            first_part_of(0)
            with act.Fori(0, TURNS - 1) as it:
                first_part_of(it + 1)
                second_part_of(it)
            second_part_of(TURNS - 1)

            act.wait_ge(bad_ready, 1)
            wide = act.value_load(bad[0:1, 0:1], min_val=0, max_val=8)
            with act.If(wide < 1):
                for x in SECTIONS:
                    with act.Fori(x.turn0, x.turn_end) as t:
                        for n in range(x.fills):
                            window, part = divmod(n, x.parts)
                            act.wait_ge(counted, x.fill(t, n + 1))
                            if n == 0:
                                act.wait_ge(applied, t + 1)
                            nc.scalar.activation(counts(x)[:, :, window, part * x.nodes:(part + 1) * x.nodes],
                                                 count_ps[n % BANKS][:, 0:x.keys].rearrange("p (t n) -> p t n", n=x.nodes),
                                                 ACT.Copy).then_inc(count_copied, 1)
            act.wait_ge(sums_ready, 1)
            def last_sums(it, u):
                act.wait_ge(node_done, it + 2 * TURNS)
                nc.scalar.activation(at2[u], acc[1][:, bass.ds(it * (Q * P), Q * P)].rearrange("p (q n) -> p q n", n=P),
                                     ACT.Copy).then_inc(copied, 1)

            with act.Fori(0, TURNS - 1, 2) as it:
                for u in range(2):
                    last_sums(it + u, u)
            last_sums(TURNS - 1, 0)

        @block.tensor
        def _(pe):
            pe.sem_inc(trans_done, 1)
            pe.sem_inc(node_done, 1)
            pe.wait_ge(weights_in, 160)
            pe.wait_ge(pool_consts, 5)
            pe.wait_ge(bounds_in, 16)
            pe.wait_ge(dve_consts, 2)
            windows = pe.alloc_register("pe_windows")
            mores = [pe.alloc_register(f"pe_more{s}") for s in range(S)]
            pe.reg_mov(windows, 0)

            def window_sum(to, parts, width, hot):
                for j in range(J):
                    for r in range(R):
                        last = nc.tensor.matmul(to[0:width, 0:W], parts[:, j, r, 0:width], hot[:, j, :],
                                                start=(j == 0 and r == 0), stop=(j == J - 1 and r == R - 1))
                return last

            def aggregate(it, s, turn, parts, width):
                g = it * S + s
                if s == 0:
                    pe.load(mores, bounds[0:1, bass.ds(g + 2 * GROUPS, S)])
                pe.nop(nofuse=True)
                more = pe.snap(mores[s], min_val=0, max_val=1)
                with pe.If(more > 0):
                    base = pe.value_load(bounds[0:1, bass.ds(g, 1)], min_val=0, max_val=NPAD - 1)
                    end = pe.value_load(bounds[0:1, bass.ds(g + GROUPS, 1)], min_val=1, max_val=NPAD)
                    with pe.Fori(base + W, end, W) as _at:
                        n = pe.snap(windows)
                        pe.wait_ge(x_onehot_done, n + 1)
                        window_sum(node_ps[:, 0, :], parts, width, x_onehot).then_inc(x_agg_done, 1)
                        pe.reg_add(windows, windows, 1)
                pe.wait_ge(onehot_done[s], after(turn))
                pe.wait_ge(added[(s - 2) % S], after(turn, -1 if s < 2 else 0))
                window_sum(agg_ps[s % 2], parts, width, onehot[s % 2]).then_inc(agg_done[s], 1)

            def hidden(it, s):
                pe.wait_ge(ea_in[s], it * 16 + 16)
                for half in range(2):
                    pe.wait_ge(relu_done[half][(s - 1) % S], after(it, -1 if s == 0 else 0))
                    cols = slice(half * HALF, (half + 1) * HALF)
                    nc.tensor.matmul(hid_ps[0:D, cols], w1t_sb[:, :], ea[s][:, cols], start=True, stop=True).then_inc(hid_done[half][s], 1)

            def edge_weights(it, s):
                pe.wait_ge(msg_done[(s - 1) % S], after(it, -1 if s == 0 else 0))
                for half in range(2):
                    pe.wait_ge(relu_done[half][s], after(it))
                    for j in range(half * J // 2, (half + 1) * J // 2):
                        last = nc.tensor.matmul(w_ps[:, j, 0:D], hid[:, j * P:(j + 1) * P], w2t_sb[:, :], start=True, stop=True)
                last.then_inc(w_done[s], 1)

            def node_products(it, before, weights, rows, cols):
                pe.wait_ge(copied, it + (before + 1))
                pe.wait_ge(node_used, it + (before + 1))
                for q in range(Q):
                    last = nc.tensor.matmul(node_ps[:, q, 0:cols], at[0:rows, q, :], weights[0:rows, 0:cols], start=True, stop=True)
                last.then_inc(node_done, 1)

            def transposes(it, u):
                pe.wait_ge(stage_done, it + 1)
                for q in range(Q):
                    last = nc.tensor.transpose(trans_ps[u][0:D1, q, :], stage[:, q, :], ident[:, :])
                last.then_inc(trans_done, 1)

            transposes(0, 0)
            with pe.Fori(0, TURNS // 2) as pair:
                it = pair * 2
                for u in range(2):
                    transposes(it + (u + 1), 1 - u)
                    node_products(it + u, 0, wst_sb, D1, D)
            node_products(TURNS - 1, 0, wst_sb, D1, D)

            def group0(it, s, ahead=2):
                if ahead >= 1:
                    edge_weights(it + (s + 1) // S, (s + 1) % S)
                if ahead >= 2:
                    hidden(it + (s + 2) // S, (s + 2) % S)
                pe.wait_ge(part2_done[s], after(it))
                pe.wait_ge(part3_done[s], after(it))
                aggregate(it, s, it, parts0[s % 2][:, :, :, :], D)

            hidden(0, 0)
            edge_weights(0, 0)
            hidden(0, 1)
            with pe.Fori(0, STEPS - 1) as it:
                for s in range(S):
                    group0(it, s)
            for s in range(S):
                group0(STEPS - 1, s, ahead=min(2, S - 1 - s))

            with pe.Fori(0, TURNS) as it:
                node_products(it, TURNS, wnt_sb, D, D)

            def gathered(it, s, turn):
                pe.wait_ge(gat_in[1][s], turn * (16 * J) + 16 * J)
                aggregate(it, s, it + STEPS, gat1[s][:, :, 0:R * D1].rearrange("p j (r d) -> p j r d", r=R), D1)

            def count(x, t, c):
                pe.wait_ge(hot_ready, x.order(t, c + 1))
                for m in range(x.units * x.parts):
                    unit, part = divmod(m, x.parts)
                    n = c * x.units * x.parts + m
                    pe.wait_ge(count_copied, x.fill(t, n + 1))
                    for j in range(x.tiles):
                        tile = unit * x.tiles + j
                        last = nc.tensor.matmul(count_ps[n % BANKS][:, 0:x.keys], low_hot(c % HOTS, tile, part * P, (part + 1) * P),
                                                key_hot(c % HOTS, tile, x.keys), start=(j == 0), stop=(j == x.tiles - 1))
                    last.then_inc(counted, 1)

            def apply(x, t):
                pe.wait_ge(count_copied, x.fill(t, x.fills + BANKS))
                pe.wait_ge(count_added, x.add(t, 1))
                for tile in range(TILES):
                    for r in range(R):
                        last = nc.tensor.matmul(applied_ps[0:D1, 0:x.adds * x.window], parts1[:, tile, r, :],
                                                counts(x)[:, tile, :, :].rearrange("p w n -> p (w n)"),
                                                start=(tile == 0 and r == 0), stop=(tile == TILES - 1 and r == R - 1))
                last.then_inc(applied, 1)

            pe.wait_ge(bad_ready, 1)
            wide = pe.value_load(bad[0:1, 0:1], min_val=0, max_val=8)
            with pe.If(wide > 0):
                with pe.Fori(0, STEPS) as it:
                    for s in range(S):
                        gathered(it, s, it)
            with pe.If(wide < 1):
                for s in range(S):
                    pe.sem_inc(agg_done[s], SKIP)
                def turn_of(x, t, last=False):
                    for s in range(S):
                        for c in range(s * x.groups // S, (s + 1) * x.groups // S):
                            count(x, t, c)
                        if last and s == S - 1:
                            apply(x, t)
                        gathered(t + SKIP, s, t)
                    if not last:
                        apply(x, t)

                for x in SECTIONS:
                    final = x is SECTIONS[-1]
                    if x.turns > 1 or not final:
                        with pe.Fori(x.turn0, x.turn_end - (1 if final else 0)) as t:
                            turn_of(x, t)
                    if final:
                        turn_of(x, x.turn_end - 1, last=True)

            def last_products(it, u):
                pe.wait_ge(copied, it + (2 * TURNS + 1))
                pe.wait_ge(node_used, it + 2 * TURNS)
                for q in range(Q):
                    last = nc.tensor.matmul(node2_ps[u][:, q, 0:D1], at2[u][:, q, :], w_sb[:, :], start=True, stop=True)
                last.then_inc(node_done, 1)

            with pe.Fori(0, TURNS - 1, 2) as it:
                for u in range(2):
                    last_products(it + u, u)
            last_products(TURNS - 1, 0)

        @block.vector
        def _(dve):
            steps = [0]

            def step(ins):
                steps[0] += 1
                ins.then_inc(dve_step, 1)
                dve.wait_ge(dve_step, steps[0])

            def center(it, layer, before):
                tiles = x_sb[:, bass.ds(it * Q, Q), :]
                mean = stat[:, 0, bass.ds(it * Q, Q)]
                nc.vector.reduce_sum(mean, tiles, axis=AX.X).then_inc(mean_step, 1)
                dve.wait_ge(mean_step, it * 2 + (layer * 2 * TURNS + 1))
                nc.vector.tensor_single_scalar(mean, mean, 1.0 / D, ALU.mult).then_inc(mean_step, 1)
                dve.wait_ge(mean_step, it * 2 + (layer * 2 * TURNS + 2))
                nc.vector.tensor_tensor(h_sb[:, bass.ds(it * Q, Q), 0:D], tiles, mean.unsqueeze(2).to_broadcast([P, Q, D]),
                                        ALU.subtract).then_inc(centered, 1)
                if before:
                    squares(it - 1, layer)

            def squares(it, layer):
                dve.wait_ge(squared, it + (layer * TURNS + 1))
                nc.vector.reduce_sum(stat[:, 1, bass.ds(it * Q, Q)], xc[:, bass.ds(it * Q, Q), :], axis=AX.X).then_inc(summed, 1)

            def variance(tiles):
                nc.vector.tensor_scalar(stat[:, 1, tiles], stat[:, 1, tiles], 1.0 / D, EPS, ALU.mult, ALU.add).then_inc(var_ready, 1)

            def inverse_deviation(tiles):
                step(nc.vector.reciprocal(stat[:, 3, tiles], stat[:, 2, tiles]))

            def normal(it):
                h = h_sb[:, bass.ds(it * Q, Q), 0:D]
                scale = stat[:, 3, bass.ds(it * Q, Q)].unsqueeze(2).to_broadcast([P, Q, D])
                nc.vector.scalar_tensor_tensor(h, h, 0.0, scale, ALU.max, ALU.mult).then_inc(normal_done, 1)

            nc.vector.memset(x_sb[:, TILES - 1, :], 0.0).then_inc(x_zeroed, 1)
            nc.vector.memset(hid[D:D1, :], 1.0).then_inc(dve_consts, 1)
            nc.vector.memset(h_sb[:, :, D:D1], 1.0)
            nc.vector.memset(w_sb[:, D:D1], 0.0).then_inc(dve_step, 1)
            steps[0] += 1
            dve.wait_ge(dve_step, steps[0])
            step(nc.vector.memset(w_sb[D:D1, D:D1], 1.0))
            dve.wait_ge(dstb_in, 16)
            halves = dst_b.rearrange("p q (u e) -> p (q u) e", u=U)
            step(nc.vector.tensor_reduce(bnd_units[:, 0, :], halves, axis=AX.X, op=ALU.min))
            step(nc.vector.tensor_reduce(bnd_units[:, 1, :], halves, axis=AX.X, op=ALU.max))
            nc.vector.tensor_single_scalar(bnd_units[:, 1, :], bnd_units[:, 1, :], 1, ALU.add).then_inc(units_ready, 1)
            dve.wait_ge(units_ready, 1)
            for n, op in enumerate((ALU.min, ALU.max)):
                step(nc.vector.tensor_reduce(bnd[:, n, :], bnd_units[:, n, :].rearrange("p (q u) -> p q u", u=U), axis=AX.X, op=op))
            step(nc.vector.tensor_tensor(bnd[:, 2, :], bnd[:, 1, :], bnd[:, 0, :], ALU.subtract))
            nc.vector.tensor_single_scalar(bnd[:, 2, :], bnd[:, 2, :], W, ALU.is_gt).then_inc(bounds_ready, 1)
            dve.wait_ge(bounds_ready, 1)
            def normal_stage(turn):
                squares(turn, 0)
                dve.wait_ge(summed, turn + 1)
                variance(slice(turn * Q, (turn + 1) * Q))

            def normal_end(turn):
                dve.wait_ge(std_ready, turn + 1)
                inverse_deviation(slice(turn * Q, (turn + 1) * Q))
                normal(turn)

            for turn in range(TURNS):
                dve.wait_ge(x_in[turn], 16 if turn < TURNS - 1 else 32)
                center(turn, 0, False)
                if turn > 0:
                    normal_stage(turn - 1)
                if turn > 1:
                    normal_end(turn - 2)
            normal_stage(TURNS - 1)
            normal_end(TURNS - 2)
            normal_end(TURNS - 1)
            dve.wait_ge(weights_in, 160)
            nc.vector.tensor_tensor(wst_sb[D:D1, :], wst_sb[D:D1, :], wnt_sb[D:D1, :], ALU.add).then_inc(dve_consts, 1)
            dve.wait_ge(dst_in, 16)
            step(nc.vector.tensor_copy(rel[:, :, :], dst_i.rearrange("p (g j) -> p g j", j=J)))
            step(nc.vector.memset(parts1_rows[:, :, R * D1:PW], 0.0))
            step(nc.vector.memset(parts1[:, :, :, D:D1], 0.0))
            step(nc.vector.memset(parts1[:, :, 0, D:D1], 1.0))
            dve.wait_ge(base_in, 16)
            step(nc.vector.tensor_copy(base_f[:, :], base_i))
            step(nc.vector.tensor_tensor(rel[:, :, :], rel[:, :, :], base_f[:, :].unsqueeze(2).to_broadcast([P, GROUPS, J]), ALU.subtract))

            dve.sem_inc(node_used, 1)
            with dve.Fori(0, TURNS) as it:
                dve.wait_ge(node_done, it + 2)
                nc.vector.tensor_copy(root[:, bass.ds(it * Q, Q), :], node_ps[:, 0:Q, 0:D]).then_inc(node_used, 1)

            dve.wait_ge(bounds_in, 16)
            dve.wait_ge(pool_consts, 5)
            dve.wait_ge(acc_ready, 2)
            dve.wait_ge(units_in, 16)
            for n, x in enumerate(SECTIONS):
                array, first = (bounds, GROUPS) if x.units == 1 else (unit_bounds, U * CG)
                g0, g1 = x.group0 * x.units, x.group_end * x.units
                step(nc.vector.tensor_tensor(spans[:, g0:g1], array[:, first + g0:first + g1], array[:, g0:g1], ALU.subtract))
                step(nc.vector.tensor_reduce(wide_f[:, n:n + 1], spans[:, g0:g1], axis=AX.X, op=ALU.max))
                step(nc.vector.tensor_single_scalar(wide_f[:, n:n + 1], wide_f[:, n:n + 1], float(x.window), ALU.is_gt))
            n = len(SECTIONS)
            step(nc.vector.reduce_sum(wide_f[:, n:n + 1], wide_f[:, 0:n], axis=AX.X))
            nc.vector.tensor_copy(bad[:, 0:1], wide_f[:, n:n + 1]).then_inc(bad_ready, 1)
            windows = dve.alloc_register("dve_windows")
            dve.reg_mov(windows, 0)
            base_before = dve.alloc_register("base_before")
            dve.sem_inc(x_added, 1)
            window = dve.alloc_register("window")
            bases = [dve.alloc_register(f"base{s}") for s in range(S)]
            mores = [dve.alloc_register(f"more{s}") for s in range(S)]
            count_bases = [dve.alloc_register(f"count_base{k}") for k in range(4)]

            def compare(to, numbers):
                return nc.vector.tensor_tensor(to[:, :, :], iota[:, :].unsqueeze(1).to_broadcast([P, J, W]),
                                               numbers.unsqueeze(2).to_broadcast([P, J, W]), ALU.is_equal)

            def add_before(turn, s, layer, width):
                b = (s - 1) % S
                wraps = -1 if s == 0 else 0
                base = dve.snap(base_before, min_val=0, max_val=NPAD - 1)
                dve.wait_ge(agg_done[b], after(turn, wraps))
                dve.wait_ge(added[(s - 2) % S], after(turn, -1 if s < 2 else 0))
                to = acc[layer][0:width, bass.ds(base, W)]
                nc.vector.tensor_tensor(to, to, agg_ps[b % 2][0:width, 0:W], ALU.add).then_inc(added[b], 1)

            def load_bounds(it):
                dve.load(bases, bounds[0:1, bass.ds(it * S, S)])
                dve.load(mores, bounds[0:1, bass.ds(it * S + 2 * GROUPS, S)])

            def further_windows(g, s, base, layer, width):
                more = dve.snap(mores[s], min_val=0, max_val=1)
                with dve.If(more > 0):
                    end = dve.value_load(bounds[0:1, bass.ds(g + GROUPS, 1)], min_val=1, max_val=NPAD)
                    dve.reg_mov(window, 1)
                    with dve.Fori(base + W, end, W) as at_node:
                        n = dve.snap(windows)
                        k = dve.snap(window, min_val=1, max_val=WMAX - 1)
                        nc.vector.tensor_scalar(x_rel[:, :], rel[:, bass.ds(g, 1), :].rearrange("p g j -> p (g j)"),
                                                shifts[:, bass.ds(k, 1)], None, ALU.subtract).then_inc(x_rel_done, 1)
                        dve.wait_ge(x_rel_done, n + 1)
                        compare(x_onehot, x_rel[:, :]).then_inc(x_onehot_done, 1)
                        dve.wait_ge(x_agg_done, n + 1)
                        dve.wait_ge(x_added, n + 1)
                        to = acc[layer][0:width, bass.ds(at_node, W)]
                        nc.vector.tensor_tensor(to, to, node_ps[0:width, 0, 0:W], ALU.add).then_inc(x_added, 1)
                        dve.reg_add(windows, windows, 1)
                        dve.reg_add(window, window, 1)
                    n = dve.snap(windows)
                    dve.wait_ge(x_added, n + 1)
                    dve.nop(nofuse=True)

            def group0(it, s, first=False):
                g = it * S + s
                if s == 0:
                    load_bounds(it)
                base = dve.snap(bases[s], min_val=0, max_val=NPAD - 1)
                compare(onehot[s % 2], rel[:, bass.ds(g, 1), :].rearrange("p g j -> p (g j)")).then_inc(onehot_done[s], 1)
                dve.wait_ge(gat_in[0][s], it * (16 * J) + 16 * J)
                dve.wait_ge(w_done[s], after(it))
                nc.vector.tensor_tensor(msg[:, :, :], w_ps[:, :, 0:D], gat0[s], ALU.mult).then_inc(msg_done[s], 1)
                if not first:
                    add_before(it, s, 0, D)
                dve.reg_mov(base_before, base)
                dve.wait_ge(part1_done[s], after(it))
                nc.vector.tensor_tensor(rest[:, :, :], msg[:, :, :], parts0[s % 2][:, :, 0, :], ALU.subtract).then_inc(rest_done[s], 1)
                dve.wait_ge(part2_done[s], after(it))
                nc.vector.tensor_tensor(parts0[s % 2][:, :, 2, :], rest[:, :, :], parts0[s % 2][:, :, 1, :], ALU.subtract).then_inc(part3_done[s], 1)
                further_windows(g, s, base, 0, D)

            def group1(it, s, first=False):
                g = it * S + s
                if s == 0:
                    load_bounds(it)
                base = dve.snap(bases[s], min_val=0, max_val=NPAD - 1)
                compare(onehot[s % 2], rel[:, bass.ds(g, 1), :].rearrange("p g j -> p (g j)")).then_inc(onehot_done[s], 1)
                if not first:
                    add_before(it + STEPS, s, 1, D1)
                dve.reg_mov(base_before, base)
                further_windows(g, s, base, 1, D1)

            for s in range(S):
                group0(0, s, first=(s == 0))
            with dve.Fori(1, STEPS) as it:
                for s in range(S):
                    group0(it, s)
            add_before(STEPS, 0, 0, D)

            def update(it, before):
                tiles = x_sb[:, bass.ds(it * Q, Q), :]
                r = root[:, bass.ds(it * Q, Q), :]
                dve.wait_ge(node_done, it + (TURNS + 2))
                nc.vector.tensor_tensor(r, node_ps[:, 0:Q, 0:D], r, ALU.add).then_inc(node_used, 1)
                dve.wait_ge(node_used, it + (TURNS + 2))
                nc.vector.scalar_tensor_tensor(tiles, r, 0.0, tiles, ALU.max, ALU.add).then_inc(x_updated, 1)
                dve.wait_ge(x_updated, it + 1)
                center(it, 1, before)

            def rest_of(it):
                dve.wait_ge(first_part, it + 1)
                nc.vector.tensor_tensor(xc[:, bass.ds(it * Q, Q), :], h_sb[:, bass.ds(it * Q, Q), 0:D],
                                        parts1[:, bass.ds(it * Q, Q), 0, 0:D], ALU.subtract).then_inc(rest_ready, 1)

            update(0, False)
            with dve.Fori(1, TURNS) as it:
                update(it, True)
            squares(TURNS - 1, 1)
            dve.wait_ge(summed, 2 * TURNS)
            variance(slice(0, TILES))
            dve.wait_ge(std_ready, TURNS + 1)
            inverse_deviation(slice(0, TILES))
            normal(0)
            with dve.Fori(0, TURNS - 1) as it:
                normal(it + 1)
                rest_of(it)
            rest_of(TURNS - 1)

            def number():
                part, node = work[1], work[2]
                whole = work[0].bitcast(I32)
                step(nc.vector.tensor_single_scalar(whole, src_i, 7, ALU.logical_shift_right))
                step(nc.vector.tensor_copy(numbers[:, :, 0, :], whole))
                step(nc.vector.tensor_single_scalar(whole, src_i, P - 1, ALU.bitwise_and))
                step(nc.vector.tensor_copy(numbers[:, :, 1, :], whole))
                step(nc.vector.tensor_copy(unit_f, unit_i))
                step(nc.vector.tensor_tensor(unit_f.rearrange("p (g u) -> p g u", u=U),
                                             base_f[:, 0:CG].unsqueeze(2).to_broadcast([P, CG, U]),
                                             unit_f.rearrange("p (g u) -> p g u", u=U), ALU.subtract))
                step(nc.vector.tensor_tensor(node.rearrange("p g (u j) -> p (g u) j", u=U),
                                             rel[:, 0:CG, :].rearrange("p g (u j) -> p (g u) j", u=U),
                                             unit_f.unsqueeze(2).to_broadcast([P, U * CG, J // U]), ALU.add))
                for x in SECTIONS:
                    groups = slice(x.group0, x.group_end)
                    n = rel[:, groups, :] if x.units == 1 else node[:, groups, :]
                    key, low, q = numbers[:, groups, 0, :], numbers[:, groups, 1, :], part[:, groups, :]
                    step(nc.vector.scalar_tensor_tensor(key, key, float(x.nodes), n, ALU.mult, ALU.add))
                    if x.parts > 1:
                        step(nc.vector.tensor_single_scalar(q, n, float(x.nodes), ALU.is_ge))
                        for k in range(2, x.parts):
                            step(nc.vector.scalar_tensor_tensor(q, n, float(k * x.nodes), q, ALU.is_ge, ALU.add))
                        step(nc.vector.scalar_tensor_tensor(low, q, float(P), low, ALU.mult, ALU.add))
                        step(nc.vector.scalar_tensor_tensor(key, q, float(-x.nodes), key, ALU.mult, ALU.add))

            def hot_rows(x, t, c, x_before, first):
                g = x.group(t, c)
                now = num_now[c % 2]
                nc.vector.tensor_copy(now[:, :, :], numbers[:, bass.ds(g, 1), :, :].rearrange("p g c j -> p (g c) j")).then_inc(num_copied, 1)
                dve.wait_ge(num_copied, x.order(t, c + 1))
                if c >= HOTS:
                    dve.wait_ge(counted, x.fill(t, (c - HOTS + 1) * x.units * x.parts))
                elif not first:
                    later = x_before.groups - 1 - max(n for n in range(x_before.groups) if n % HOTS == c)
                    dve.wait_ge(counted, x.fill(t, -later * x_before.units * x_before.parts))
                for j in range(J):
                    nc.vector.tensor_scalar(key_hot(c % HOTS, j, x.keys), iota16[:, 0:x.keys], now[:, 0, j:j + 1], None, ALU.is_equal)
                    last = nc.vector.tensor_scalar(low_hot(c % HOTS, j, 0, x.parts * P), iota16[:, 0:x.parts * P], now[:, 1, j:j + 1],
                                                   None, ALU.is_equal)
                last.then_inc(hot_ready, 1)

            def add_counted(x, t, s, blocks):
                turn = t + (SKIP + STEPS)
                dve.wait_ge(applied, t + 1)
                dve.wait_ge(added[(s - 2) % S], after(turn, -1 if s < 2 else 0))
                array = bounds if x.units == 1 else unit_bounds
                first = t * x.adds + ((x.group0 - x.turn0 * x.groups) * x.units - x.adds)
                for block in blocks:
                    dve.load(count_bases, array[0:1, bass.ds(first + block * 4, 4)])
                    for k in range(4):
                        n = block * 4 + k
                        base = dve.snap(count_bases[k], min_val=0, max_val=NPAD - 1)
                        dve.wait_ge(count_added, x.add(t, n + 1 - x.adds))
                        to = acc[1][:, bass.ds(base, x.window)]
                        nc.vector.tensor_tensor(to, to, applied_ps[0:D1, n * x.window:(n + 1) * x.window], ALU.add).then_inc(count_added, 1)
                dve.wait_ge(count_added, x.add(t, (blocks[-1] + 1) * 4 + 1 - x.adds))
                dve.nop(nofuse=True)

            def both(x, t, x_before, first=False):
                for s in range(S):
                    for c in range(s * x.groups // S, (s + 1) * x.groups // S):
                        hot_rows(x, t, c, x_before, first)
                    if not first:
                        total = x_before.adds // 4
                        blocks = range(total)[(s - 1) * total // (S - 1):s * total // (S - 1)] if s > 0 else ()
                        if len(blocks) > 0:
                            add_counted(x_before, t, s, blocks)
                    group1(t + SKIP, s, first=(first and s == 0))

            dve.wait_ge(src_in, 16)
            dve.wait_ge(unit_in, 16)
            dve.wait_ge(bad_ready, 1)
            wide = dve.value_load(bad[0:1, 0:1], min_val=0, max_val=8)
            with dve.If(wide > 0):
                for s in range(S):
                    group1(0, s, first=(s == 0))
                with dve.Fori(1, STEPS) as it:
                    for s in range(S):
                        group1(it, s)
                add_before(2 * STEPS, 0, 1, D1)
            with dve.If(wide < 1):
                for s in range(S):
                    dve.sem_inc(onehot_done[s], SKIP)
                    dve.sem_inc(added[s], SKIP)
                dve.wait_ge(table_ready, TURNS)
                number()
                before = None
                for x in SECTIONS:
                    both(x, x.turn0, before, first=(before is None))
                    if x.turns > 1:
                        with dve.Fori(x.turn0 + 1, x.turn_end) as t:
                            both(x, t, x)
                    before = x
                add_counted(before, TURNS1, 0, range(before.adds // 4))
                add_before(2 * STEPS, 0, 1, D1)
            dve.wait_ge(added[S - 1], after(2 * STEPS - 1))
            dve.sem_inc(sums_ready, 1)

            def output(it, u):
                o = xc[:, bass.ds(it * Q, Q), :]
                deg = stat[:, 0, 0:Q]
                inv = stat[:, 1, 0:Q]
                dve.wait_ge(node_done, it + (2 * TURNS + 2))
                nc.vector.tensor_single_scalar(deg, node2_ps[u][:, 0:Q, D], 1.0, ALU.max).then_inc(scaled, 1)
                dve.wait_ge(scaled, it * 3 + 1)
                nc.vector.reciprocal(inv, deg).then_inc(scaled, 1)
                dve.wait_ge(scaled, it * 3 + 2)
                nc.vector.tensor_tensor(o, node2_ps[u][:, 0:Q, 0:D], inv.unsqueeze(2).to_broadcast([P, Q, D]), ALU.mult).then_inc(scaled, 1)
                dve.wait_ge(scaled, it * 3 + 3)
                dve.sem_inc(node_used, 1)
                nc.vector.tensor_tensor(o, o, x_sb[:, bass.ds(it * Q, Q), :], ALU.add).then_inc(out_ready, 1)

            with dve.Fori(0, TURNS - 1, 2) as it:
                for u in range(2):
                    output(it + u, u)
            output(TURNS - 1, 0)


def kernel(x, src, dst, edge_attr_17, L0_gnn_W1, L0_gnn_b1, L0_gnn_W2, L0_gnn_b2, L0_gnn_Ws, L0_gnn_bs,
           L0_gnn_Wn, L0_gnn_bn, L1_gnn_W, L1_gnn_b):
    import numpy as np
    import concourse.bacc as bacc
    from concourse.bass_utils import run_bass_kernel_spmd

    def padded(a, fill):
        return np.concatenate([np.asarray(a), np.full((EPAD - E, *a.shape[1:]), fill, np.asarray(a).dtype)])

    src_p = padded(src, 0).reshape(GROUPS, J, P)
    dst_p = padded(dst, NPAD - 1)
    ea_p = padded(edge_attr_17, 0).reshape(GROUPS, GE, DE)
    arrays = {
        "x": x,
        "src_ids": src_p.transpose(0, 2, 1),
        "src_cols": src_p.reshape(GROUPS * J, P).T[:, 0:CG * J],
        "dst_ids": dst_p.reshape(GROUPS * J, P).T,
        "dst_flat": dst_p,
        "edge_attr": ea_p.transpose(0, 2, 1),
        "w1t": np.asarray(L0_gnn_W1).T, "b1": np.asarray(L0_gnn_b1).reshape(D, 1),
        "w2t": np.asarray(L0_gnn_W2).T, "b2": np.asarray(L0_gnn_b2).reshape(1, D),
        "wst": np.asarray(L0_gnn_Ws).T, "bs": np.asarray(L0_gnn_bs).reshape(1, D),
        "wnt": np.asarray(L0_gnn_Wn).T, "bn": np.asarray(L0_gnn_bn).reshape(1, D),
        "w": L1_gnn_W, "b": np.asarray(L1_gnn_b).reshape(1, D),
    }
    nc = bacc.Bacc("TRN2", target_bir_lowering=False, num_devices=1)
    arrays = {k: np.ascontiguousarray(v) for k, v in arrays.items()}
    aps = [nc.dram_tensor(k, v.shape, mybir.dt.from_np(v.dtype), kind="ExternalInput").ap() for k, v in arrays.items()]
    out = nc.dram_tensor("out", (N, D), F32, kind="ExternalOutput").ap()
    gnn_program(nc, *aps, out)
    return run_bass_kernel_spmd(nc, [arrays], core_ids=[0]).results[0]["out"]
```
